# Optimizing a Trainium2 kernel written in Bass

```python
import numpy as np
import jax
import jax.numpy as jnp

def _softmax(x, axis=-1):
    return jax.nn.softmax(x, axis=axis)

def _gelu(x):
    return jax.nn.gelu(x, approximate=True)

def _silu(x):
    return jax.nn.silu(x)

def _sigmoid(x):
    return jax.nn.sigmoid(x)

def _layernorm(x, axis=-1, eps=1e-05):
    m = jnp.mean(x, axis=axis, keepdims=True)
    v = jnp.var(x, axis=axis, keepdims=True)
    return (x - m) / jnp.sqrt(v + eps)

def _scatter_add(tgt, idx, src, axis=0):
    return tgt.at[idx].add(src)

def _segment_sum(src, seg, n):
    return jax.ops.segment_sum(src, seg, n)
kernel_name = 'mk_hybrid_d1_jaxref_r4_acd0be'

def setup_inputs(seed: int=0):
    np.random.seed(seed)
    _w = jnp.asarray

    def _L0_attn_a_setup():
        import jax, jax.numpy as jnp
        import numpy as np
        DIM = 256
        NUM_HEADS = 16
        HEAD_DIM = DIM // NUM_HEADS
        B, L = (4, 512)

        def _alibi_bias_causal(seq_len, dtype):
            h = jnp.arange(1, NUM_HEADS + 1, dtype=jnp.float32)
            slopes = jnp.power(2.0, -8.0 * h / NUM_HEADS)
            pos = jnp.arange(seq_len, dtype=jnp.float32)
            rel = jnp.abs(pos[:, None] - pos[None, :])
            bias = -slopes[:, None, None] * rel[None, :, :]
            causal = pos[:, None] >= pos[None, :]
            bias = jnp.where(causal[None, :, :], bias, -jnp.inf)
            return bias.astype(dtype)
        key = jax.random.key(seed)
        ks = jax.random.split(key, 9)
        s = 0.02
        return {'x': jax.random.normal(ks[0], (B, L, DIM), jnp.float32), 'Wq': jax.random.normal(ks[1], (DIM, DIM), jnp.float32) * s, 'bq': jax.random.normal(ks[2], (DIM,), jnp.float32) * s, 'Wk': jax.random.normal(ks[3], (DIM, DIM), jnp.float32) * s, 'bk': jax.random.normal(ks[4], (DIM,), jnp.float32) * s, 'Wv': jax.random.normal(ks[5], (DIM, DIM), jnp.float32) * s, 'bv': jax.random.normal(ks[6], (DIM,), jnp.float32) * s, 'Wo': jax.random.normal(ks[7], (DIM, DIM), jnp.float32) * s, 'bo': jax.random.normal(ks[8], (DIM,), jnp.float32) * s}
    _L0_attn_a_in = _L0_attn_a_setup()

    def _L0_attn_b_setup():
        import jax, jax.numpy as jnp
        import numpy as np
        from math import sqrt
        D_MODEL = 256
        NUM_HEADS = 16
        D_HEAD = D_MODEL // NUM_HEADS
        THETA = 10000.0

        def _rope(x, freqs):
            xr = x[..., ::2]
            xi = x[..., 1::2]
            cos = jnp.cos(freqs)
            sin = jnp.sin(freqs)
            yr = xr * cos - xi * sin
            yi = xr * sin + xi * cos
            return jnp.stack([yr, yi], axis=-1).reshape(x.shape)
        key = jax.random.key(seed)
        k1, k2, k3 = jax.random.split(key, 3)
        X = jax.random.normal(k1, (4, 512, D_MODEL), dtype=jnp.float32)
        std_kqv = sqrt(2.0 / (D_MODEL + 3 * D_MODEL))
        W_KQV = std_kqv * jax.random.truncated_normal(k2, -3.0, 3.0, (3 * D_MODEL, D_MODEL), dtype=jnp.float32)
        std_o = sqrt(2.0 / (D_MODEL + D_MODEL))
        W_O = std_o * jax.random.truncated_normal(k3, -3.0, 3.0, (D_MODEL, D_MODEL), dtype=jnp.float32)
        return {'X': X, 'W_KQV': W_KQV, 'W_O': W_O}
    _L0_attn_b_in = _L0_attn_b_setup()

    def _L0_ffn_setup():
        import jax, jax.numpy as jnp
        import numpy as np
        SL, BS, HS, FF, E, TOPK = (512, 2, 256, 1024, 8, 2)
        key = jax.random.key(seed)
        ks = jax.random.split(key, 6)
        T = SL * BS
        x = jax.random.normal(ks[0], (SL, BS, HS), jnp.float32)
        scores = jax.random.uniform(ks[1], (T, E), jnp.float32)
        expert_weights = jax.random.uniform(ks[2], (T, TOPK), jnp.float32)
        expert_indices = jax.random.randint(ks[3], (T, TOPK), 0, E, jnp.int32)
        w1 = jax.random.normal(ks[4], (E, HS, FF), jnp.float32) * (1.0 / np.sqrt(HS))
        w2 = jax.random.normal(ks[5], (E, FF, HS), jnp.float32) * (1.0 / np.sqrt(FF))
        bias = jnp.zeros((HS,), jnp.float32)
        return dict(x=x, scores=scores, expert_weights=expert_weights, expert_indices=expert_indices, w1=w1, w2=w2, bias=bias)
    _L0_ffn_in = _L0_ffn_setup()
    _d = {'L0_attn_a_x': _L0_attn_a_in['x'], 'L0_attn_a_Wq': _L0_attn_a_in['Wq'], 'L0_attn_a_bq': _L0_attn_a_in['bq'], 'L0_attn_a_Wk': _L0_attn_a_in['Wk'], 'L0_attn_a_bk': _L0_attn_a_in['bk'], 'L0_attn_a_Wv': _L0_attn_a_in['Wv'], 'L0_attn_a_bv': _L0_attn_a_in['bv'], 'L0_attn_a_Wo': _L0_attn_a_in['Wo'], 'L0_attn_a_bo': _L0_attn_a_in['bo'], 'L0_attn_b_W_KQV': _L0_attn_b_in['W_KQV'], 'L0_attn_b_W_O': _L0_attn_b_in['W_O'], 'L0_ffn_scores': _L0_ffn_in['scores'], 'L0_ffn_expert_weights': _L0_ffn_in['expert_weights'], 'L0_ffn_expert_indices': _L0_ffn_in['expert_indices'], 'L0_ffn_w1': _L0_ffn_in['w1'], 'L0_ffn_w2': _L0_ffn_in['w2'], 'L0_ffn_bias': _L0_ffn_in['bias']}
    _x0 = _d['L0_attn_a_x']
    _d['L0_attn_a_x'] = jax.random.normal(jax.random.fold_in(jax.random.key(seed), 1), (4, 2048, 256), dtype=_x0.dtype)
    del _x0
    return _d

def reference(L0_attn_a_x, L0_attn_a_Wq, L0_attn_a_bq, L0_attn_a_Wk, L0_attn_a_bk, L0_attn_a_Wv, L0_attn_a_bv, L0_attn_a_Wo, L0_attn_a_bo, L0_attn_b_W_KQV, L0_attn_b_W_O, L0_ffn_scores, L0_ffn_expert_weights, L0_ffn_expert_indices, L0_ffn_w1, L0_ffn_w2, L0_ffn_bias):

    def _L0_attn_a_ref(x, Wq, bq, Wk, bk, Wv, bv, Wo, bo):
        import jax, jax.numpy as jnp
        import numpy as np
        DIM = 256
        NUM_HEADS = 16
        HEAD_DIM = DIM // NUM_HEADS
        B, L = (4, 512)

        def _alibi_bias_causal(seq_len, dtype):
            h = jnp.arange(1, NUM_HEADS + 1, dtype=jnp.float32)
            slopes = jnp.power(2.0, -8.0 * h / NUM_HEADS)
            pos = jnp.arange(seq_len, dtype=jnp.float32)
            rel = jnp.abs(pos[:, None] - pos[None, :])
            bias = -slopes[:, None, None] * rel[None, :, :]
            causal = pos[:, None] >= pos[None, :]
            bias = jnp.where(causal[None, :, :], bias, -jnp.inf)
            return bias.astype(dtype)
        b, l, d = x.shape
        q = (jnp.einsum('bld,ed->ble', x, Wq) + bq).reshape(b, l, NUM_HEADS, HEAD_DIM).transpose(0, 2, 1, 3)
        k = (jnp.einsum('bld,ed->ble', x, Wk) + bk).reshape(b, l, NUM_HEADS, HEAD_DIM).transpose(0, 2, 1, 3)
        v = (jnp.einsum('bld,ed->ble', x, Wv) + bv).reshape(b, l, NUM_HEADS, HEAD_DIM).transpose(0, 2, 1, 3)
        scale = 1.0 / np.sqrt(HEAD_DIM)
        scores = jnp.einsum('bhqd,bhkd->bhqk', q, k) * scale
        scores = scores + _alibi_bias_causal(l, scores.dtype)[None]
        attn = jax.nn.softmax(scores, axis=-1)
        out = jnp.einsum('bhqk,bhkd->bhqd', attn, v)
        out = out.transpose(0, 2, 1, 3).reshape(b, l, d)
        return jnp.einsum('bld,ed->ble', out, Wo) + bo

    def _L0_attn_b_ref(X, W_KQV, W_O):
        import jax, jax.numpy as jnp
        import numpy as np
        from math import sqrt
        D_MODEL = 256
        NUM_HEADS = 16
        D_HEAD = D_MODEL // NUM_HEADS
        THETA = 10000.0

        def _rope(x, freqs):
            xr = x[..., ::2]
            xi = x[..., 1::2]
            cos = jnp.cos(freqs)
            sin = jnp.sin(freqs)
            yr = xr * cos - xi * sin
            yi = xr * sin + xi * cos
            return jnp.stack([yr, yi], axis=-1).reshape(x.shape)
        B, S, D = X.shape
        H, d = (NUM_HEADS, D_HEAD)
        KQV = jnp.einsum('bsd,ed->bse', X, W_KQV)
        K, Q, V = jnp.split(KQV, [D, 2 * D], axis=-1)

        def to_heads(t):
            return t.reshape(B, S, H, d).transpose(0, 2, 1, 3)
        K, Q, V = (to_heads(K), to_heads(Q), to_heads(V))
        inv_freq = 1.0 / THETA ** (jnp.arange(0, d, 2, dtype=jnp.float32) / d)
        pos = jnp.arange(S, dtype=jnp.float32)
        freqs = pos[:, None] * inv_freq[None, :]
        Q = _rope(Q, freqs)
        K = _rope(K, freqs)
        scores = jnp.einsum('bhqd,bhkd->bhqk', Q, K) / sqrt(d)
        causal = jnp.triu(jnp.ones((S, S), dtype=bool), k=1)
        scores = jnp.where(causal, -jnp.inf, scores)
        probs = jax.nn.softmax(scores, axis=-1)
        heads = jnp.einsum('bhqk,bhkd->bhqd', probs, V)
        acts = heads.transpose(0, 2, 1, 3).reshape(B, S, D)
        return jnp.einsum('bsd,ed->bse', acts, W_O)

    def _L0_ffn_ref(x, scores, expert_weights, expert_indices, w1, w2, bias):
        import jax, jax.numpy as jnp
        import numpy as np
        SL, BS, HS, FF, E, TOPK = (512, 2, 256, 1024, 8, 2)
        sl, bs, hs = x.shape
        n_exp = w1.shape[0]
        top_k = expert_indices.shape[-1]
        xf = x.reshape(-1, hs)
        flat_idx = expert_indices.reshape(-1)
        flat_w = expert_weights.reshape(-1)
        order = jnp.argsort(flat_idx)
        tok = order // top_k
        tokens_per_expert = jnp.bincount(flat_idx, length=n_exp).astype(jnp.int32)
        xs = xf[tok]
        h = jax.nn.gelu(jax.lax.ragged_dot(xs, w1, tokens_per_expert), approximate=False)
        ys = jax.lax.ragged_dot(h, w2, tokens_per_expert)
        ys = ys * flat_w[order][:, None]
        out = jnp.zeros_like(xf).at[tok].add(ys)
        return out.reshape(sl, bs, hs) + bias
    x = L0_attn_a_x
    x = x + _L0_attn_a_ref(_layernorm(x, axis=-1), L0_attn_a_Wq, L0_attn_a_bq, L0_attn_a_Wk, L0_attn_a_bk, L0_attn_a_Wv, L0_attn_a_bv, L0_attn_a_Wo, L0_attn_a_bo)
    x = x + _L0_ffn_ref(_layernorm(x, axis=-1), L0_ffn_scores, L0_ffn_expert_weights, L0_ffn_expert_indices, L0_ffn_w1, L0_ffn_w2, L0_ffn_bias)
    x = x + _L0_attn_b_ref(_layernorm(x, axis=-1), L0_attn_b_W_KQV, L0_attn_b_W_O)
    x = x + _L0_ffn_ref(_layernorm(x, axis=-1), L0_ffn_scores, L0_ffn_expert_weights, L0_ffn_expert_indices, L0_ffn_w1, L0_ffn_w2, L0_ffn_bias)
    return x

_drawn_inputs = setup_inputs


def setup_inputs(seed=0):
    import zlib

    import numpy as np

    out = dict(_drawn_inputs(seed))
    spreads = {'L0_ffn_bias': (0.0, 0.1)}
    factors = {'L0_attn_a_Wq': 8.0,
     'L0_attn_a_bq': 40.377,
     'L0_attn_a_Wk': 8.0,
     'L0_attn_a_bk': 64.0,
     'L0_attn_a_bv': 7.906,
     'L0_attn_a_bo': 2.684}
    for name, (base, spread) in spreads.items():
        noise = np.random.default_rng([zlib.crc32(name.encode()), seed]).standard_normal(out[name].shape)
        drawn = base * np.exp(spread * noise) if base else spread * noise
        out[name] = jnp.asarray(drawn.astype(out[name].dtype))
    for name, factor in factors.items():
        out[name] = (out[name] * factor).astype(out[name].dtype)
    return out
```

```python
from contextlib import ExitStack

import numpy as np

import concourse.bass as bass
from concourse import mybir

F32 = mybir.dt.float32
BF16 = mybir.dt.bfloat16
I32 = mybir.dt.int32
ALU = mybir.AluOpType
ACT = mybir.ActivationFunctionType
AX_X = mybir.AxisListType.X

P = 128
B, L, D = 4, 2048, 256
H, DH = 16, 16
KD = D // P
TT = L // P
QW = 512
NQ = L // QW
E, FF, TOPK = 8, 1024, 2
FT = 1024
NFT = FT // P
NF = FF // P
EPS = 1e-5
MASKED = -1e30
LOWEST = -3.0e38

SLOTS = 4
GROUP = 4
NPART = 6
Q_PARTS = (0, 0, 0, 1, 1, 2)
K_PARTS = (0, 1, 2, 0, 1, 0)
POS = 12

CHUNKS = sum(2 * (qt + 1) for qt in range(NQ))
UNITS = sum(4 * (qt + 1) for qt in range(NQ))
LOADS = 2 * NPART
CONSTS = 16 * 12


def chunk_list():
    out = []
    for qt in reversed(range(NQ)):
        for c in range(2 * (qt + 1)):
            blocks, at = [], 0
            for kb in (2 * c, 2 * c + 1):
                r = kb - 4 * qt
                first = P * r if r > 0 else 0
                blocks.append((kb, first, QW - first, at))
                at += QW - first
            out.append((qt, c, blocks))
    return out


def unit_list():
    out = []
    for qt in reversed(range(NQ)):
        for qb in range(4 * qt, 4 * qt + 4):
            for kc in range(qt + 1):
                out.append((qb, kc, QW if kc < qt else P * (qb - 4 * qt + 1)))
    return out


CHUNK = chunk_list()
UNIT = unit_list()
HI_UNITS = sum(1 for qb, _, _ in UNIT if qb >= TT // 2)
LO, HI = -1, -2


def stream(with_next):
    return [([LO] if n == 2 else []) + ([2 * n, 2 * n + 1] if with_next else []) +
            ([HI] if with_next and n == 16 else []) for n in range(CHUNKS)]


FIRST_STREAM = list(range(UNITS)) + [HI]
ITEMS = UNITS + 2
LAST_GROUP = {3: 3, 6: 2, 8: 1, 9: 0}
FIRST_GROUP = {0: 3, 4: 2, 7: 1, 9: 0}


def build(nc, x_in, w_a, wo_a, bqk_a, bv_a, bo_a, w_b, wo_b, cos_t, sin_t, q_pos, k_pos, ones_rows,
          ident_in, mask_in, sel_in, e_w, e_idx, w1, w2, fbias, out):
    x_a = nc.dram_tensor("x_after_a", (B * L, D), F32, kind="Internal").ap()
    x_b = nc.dram_tensor("x_after_b", (B * L, D), F32, kind="Internal").ap()

    def tiles(ap):
        return ap.rearrange("(b t p) d -> p b t d", p=P, t=TT)

    with ExitStack() as ctx:
        def sb(name, shape, dt=F32):
            return ctx.enter_context(nc.sbuf_tensor(name, shape, dt))

        def sem(name):
            return ctx.enter_context(nc.semaphore(name))

        xb = sb("xb", [P, TT, D])
        xT = sb("xT", [P, KD, L])
        oh = sb("oh", [P, TT, D])
        parts_f = sb("parts", [P, 12 * L // 2])
        stack_f = sb("stacks", [P, 2 * SLOTS * L // 2])
        v_all = sb("v_all", [P, TT, D])
        v_head = sb("v_head", [P, 2, TT, 2 * DH])
        probs = sb("probs", [P, 4, 2 * QW])
        acc_sb = sb("acc_sb", [P, 2, QW])
        wqkv = sb("wqkv", [P, KD, 5 * D])
        wo = sb("wo", [P, KD, D])
        cosb = sb("cosb", [P, L])
        sinb = sb("sinb", [P, L])
        bv_bc = sb("bv_bc", [P, D])
        bo_bc = sb("bo_bc", [P, D])
        fb_bc = sb("fb_bc", [P, D])
        bqk = sb("bqk", [P, 2, KD])
        identf = sb("identf", [P, P])
        identb = sb("identb", [P, P], BF16)
        masks = sb("masks", [P, 2, P], BF16)
        sel = sb("sel", [P, DH + 1])
        zeros = sb("zeros", [P, QW], BF16)
        xn = sb("xn", [P, 4, D])
        stats = sb("stats", [P, TT, 6])
        mv = sb("mv", [P, TT, 2])
        vpe = sb("vpe", [P, TT])
        sd = sb("sd", [P, TT])
        r0 = sb("r0", [P, TT])
        r1 = sb("r1", [P, TT])
        rstd = sb("rstd", [P, TT])
        part_max = sb("part_max", [P, TT, NQ])
        negmax = sb("negmax", [P, TT])
        cres = sb("cres", [P, 2, TT // 2])
        cpart = sb("cpart", [P, 2, 3, TT // 2], BF16)
        crow = sb("crow", [3 * TT // 2, 2, P], BF16)
        recip = sb("recip", [P, TT])
        ewt = sb("ewt", [P, NFT, TOPK])
        eix = sb("eix", [P, NFT, TOPK], I32)
        eixf = sb("eixf", [P, NFT, TOPK])
        wtok = sb("wtok", [P, E, NFT])

        parts = parts_f[:, :].bitcast(BF16).rearrange("p (a n) -> p a n", n=L)
        stacks = stack_f[:, :].bitcast(BF16).rearrange("p (a n) -> p a n", n=L)
        qf = probs[:, 0, :].rearrange("p (a n) -> p a n", a=2)
        res = probs[:, 1, :].rearrange("p (a n) -> p a n", a=2)
        rot1 = probs[:, 2, :].rearrange("p (a n) -> p a n", a=2)
        rot2 = probs[:, 3, :].rearrange("p (a n) -> p a n", a=2)
        epick = probs[:, 0, 0:E * NFT * TOPK].rearrange("p (e t k) -> p e t k", e=E, t=NFT)
        o_t = acc_sb[:, :, 0:D]
        w1_sb = stack_f[:, 0:2 * KD * FF].rearrange("p (s k f) -> p s k f", s=2, k=KD)
        w2_sb = stack_f[:, 2 * KD * FF:].rearrange("p (s f d) -> p s f d", s=2, f=NF)
        hid = parts_f[:, 0:2 * NF * QW].rearrange("p (s f n) -> p s f n", s=2, f=NF)
        facc = oh[:, 0:NFT, :]

        def part(proj, half, i):
            return parts[:, (proj * KD + half) * 3 + i, :]

        def q_stack(s):
            return stacks[:, 2 * s, :]

        def k_stack(s):
            return stacks[:, 2 * s + 1, :]

        ps_s = ctx.enter_context(nc.psum_tensor("ps_s", [P, 2, 2 * QW], F32))
        ps_m = ctx.enter_context(nc.psum_tensor("ps_m", [P, 2, QW], F32))
        ps_acc = ctx.enter_context(nc.psum_tensor("ps_acc", [P, QW], F32))
        ps_o = ctx.enter_context(nc.psum_tensor("ps_o", [P, QW], F32))
        ring = ps_s[:, :, :].rearrange("p a (c n) -> p (a c) n", n=QW)
        o_ps = ps_o[:, 0:TT * (DH + 1)].rearrange("p (t d) -> p t d", d=DH + 1)
        c_ps = [ps_m[:, i, 0:P // 2].bitcast(BF16) for i in range(2)]

        passed = sem("passed")
        consts_in = sem("consts_in")
        weights_in = sem("weights_in")
        x_in_sb = sem("x_in_sb")
        x_stored = sem("x_stored")
        ones_in = sem("ones_in")
        bq_scaled = sem("bq_scaled")
        stack_in = [sem(f"stack_in{s}") for s in range(SLOTS)]
        rows_in = [[sem(f"rows_in{g}{s}") for s in range(SLOTS)] for g in range(2)]
        dve_step = sem("dve_step")
        pool_step = sem("pool_step")
        var_ready = sem("var_ready")
        sd_ready = sem("sd_ready")
        xn_ready = sem("xn_ready")
        xn_turned = sem("xn_turned")
        xT_ready = sem("xT_ready")
        v_mm = sem("v_mm")
        v_ready = sem("v_ready")
        qk_mm = sem("qk_mm")
        rotated = sem("rotated")
        roped = sem("roped")
        qk_out = sem("qk_out")
        qk_split = sem("qk_split")
        item_mm = sem("item_mm")
        item_used = sem("item_used")
        m_ready = sem("m_ready")
        c_ready = sem("c_ready")
        v_head_ready = sem("v_head_ready")
        s_mm = sem("s_mm")
        exp_done = sem("exp_done")
        pv_mm = sem("pv_mm")
        acc_out = sem("acc_out")
        o_mm = sem("o_mm")
        o_norm = sem("o_norm")
        stack_free = sem("stack_free")
        ot_mm = sem("ot_mm")
        ot_out = sem("ot_out")
        y_mm = sem("y_mm")
        y_added = sem("y_added")
        x_ready = sem("x_ready")
        facc_zero = sem("facc_zero")
        ew_in = [sem("ew_in0"), sem("ew_in1")]
        h_mm = sem("h_mm")
        gelu_out = sem("gelu_out")
        fy_mm = sem("fy_mm")
        fy_added = sem("fy_added")

        prod_row = (POS, 0)
        c_row = (POS + 16 * NPART, 16 * NPART)

        assert H == TT == 4 * NQ

        def upto(per, ly, b16, n, more=0):
            return b16 * per + (per * (ly * B * H + n) + more)

        def item_count(ly, hb, h, at):
            if h is None:
                return upto(ITEMS, ly, hb, 0, at)
            return upto(ITEMS, ly, hb, h, len(FIRST_STREAM) + at)

        def ln_tile(ly, b16, n):
            return b16 + (ly * (B * TT + NFT) + n)

        block = ctx.enter_context(nc.Block())

        @block.sync
        def _(sp):
            for dst, src in ((identf[:, :], ident_in[0]), (identb[:, :], ident_in[1]), (masks[:, :, :], mask_in),
                             (sel[:, :], sel_in), (bv_bc[:, :], bv_a), (bo_bc[:, :], bo_a), (fb_bc[:, :], fbias),
                             (bqk[:, :, :], bqk_a), (cosb[:, :], cos_t), (sinb[:, :], sin_t),
                             (ewt[:, :, :], e_w.rearrange("(t p) k -> p t k", p=P)),
                             (eix[:, :, :], e_idx.rearrange("(t p) k -> p t k", p=P))):
                sp.dma_start(dst, src).then_inc(consts_in, 16)

            def weights(ly):
                w, w_o = ((w_a, wo_a), (w_b, wo_b))[ly]
                n = w.shape[1]
                sp.dma_start(wqkv[:, :, 0:n], w.rearrange("(k p) n -> p k n", p=P)).then_inc(weights_in, 16)
                sp.dma_start(wo[:, :, :], w_o.rearrange("(k p) n -> p k n", p=P)).then_inc(weights_in, 16)
                for s in range(SLOTS):
                    sp.dma_start(k_stack(s)[c_row[ly]:c_row[ly] + 3, :], ones_rows).then_inc(ones_in, 16)

            def load_stack(ly, b16, h):
                s = h % SLOTS
                half, r = h // 8, 16 * (h % 8)
                sp.wait_ge(stack_free, upto(1, ly, b16, h, 1))
                sp.sem_inc(passed, 1)
                if h % 8 == 0:
                    sp.wait_ge(qk_split, upto(1, ly, b16, 8 * half + 8))
                for stack, source, proj in ((q_stack(s), Q_PARTS, 0), (k_stack(s), K_PARTS, 1)):
                    for g, i in enumerate(source):
                        to = prod_row[ly] + 16 * g
                        sp.dma_start(stack[to:to + 16, :], part(proj, half, i)[r:r + 16, :]).then_inc(stack_in[s], 16)
                if ly == 0:
                    sp.dma_start(q_stack(s)[0:POS, :], q_pos[h]).then_inc(stack_in[s], 16)
                    sp.dma_start(k_stack(s)[0:POS, :], k_pos[h]).then_inc(stack_in[s], 16)

            def load_rows(ly, b16, h, g):
                s = h % SLOTS
                first = (TT // 2 * P, 0)[g]
                if g:
                    before = item_count(ly, b16, h, 4 if h + 1 < H else 0)
                elif h == 0:
                    before = item_count(ly, b16, None, UNITS)
                else:
                    before = item_count(ly, b16, h - 1, 2 * 17 + 1)
                sp.wait_ge(item_used, before + 1)
                for i in range(3):
                    row = q_stack(s)[c_row[ly] + i:c_row[ly] + i + 1, first:first + TT // 2 * P]
                    sp.dma_start(row, crow[TT // 2 * i:TT // 2 * (i + 1), g, :]).then_inc(rows_in[g][s], 16)

            for ly in range(2):
                weights(ly)
                x_from = (x_in, x_a)[ly]
                with sp.Fori(0, B) as b:
                    b16 = b * TT
                    sp.dma_start(xb[:, :, :], tiles(x_from)[:, bass.ds(b, 1), :, :].rearrange("p o t d -> p (o t) d"))\
                        .then_inc(x_in_sb, 16)
                    load_stack(ly, b16, 0)
                    load_stack(ly, b16, 1)
                    load_stack(ly, b16, 2)
                    load_rows(ly, b16, 0, 0)
                    load_rows(ly, b16, 0, 1)
                    for h in range(H):
                        if h + 3 < H:
                            load_stack(ly, b16, h + 3)
                        if h + 1 < H:
                            load_rows(ly, b16, h + 1, 0)
                            load_rows(ly, b16, h + 1, 1)
                    sp.wait_ge(x_ready, ln_tile(ly, b16, TT))
                    sp.sem_inc(passed, 1)
                    to = (x_a, x_b)[ly]
                    sp.dma_start(tiles(to)[:, bass.ds(b, 1), :, :].rearrange("p o t d -> p (o t) d"), xb[:, :, :])\
                        .then_inc(x_stored, 16)
                    if ly:
                        sp.dma_start(tiles(out)[:, bass.ds(b, 1), :, :].rearrange("p o t d -> p (o t) d"),
                                     xT[:, :, :].rearrange("p k n -> p (k n)").rearrange("p (t d) -> p t d", d=D))\
                            .then_inc(x_stored, 16)
                    sp.wait_ge(x_stored, (16 * (b + 1) if ly == 0 else 16 * (B + 1) + 32 * (b + 1)))
                    sp.sem_inc(passed, 1)
                src = (x_a, x_b)[ly][0:FT, :].rearrange("(t p) d -> p t d", p=P)
                sp.dma_start(xb[:, 0:NFT, :], src).then_inc(x_in_sb, 16)
                with sp.Fori(0, E // 2) as ep:
                    for s in range(2):
                        sp.wait_ge(fy_mm, ly * E * NFT + ep * 2 * NFT + s * NFT + 1)
                        sp.sem_inc(passed, 1)
                        sp.dma_start(w1_sb[:, s, :, :], w1[bass.ds(2 * ep + s, 1), :, :]
                                     .rearrange("o (k p) f -> p (o k) f", p=P)).then_inc(ew_in[s], 16)
                        sp.dma_start(w2_sb[:, s, :, :], w2[bass.ds(2 * ep + s, 1), :, :]
                                     .rearrange("o (f p) d -> p (o f) d", p=P)).then_inc(ew_in[s], 16)
                sp.wait_ge(x_ready, ln_tile(ly, B * TT, NFT))
                to = (x_a, out)[ly][0:FT, :].rearrange("(t p) d -> p t d", p=P)
                sp.dma_start(to, xb[:, 0:NFT, :]).then_inc(x_stored, 16)
                sp.wait_ge(x_stored, (16 * (B + 1), 16 * (B + 1) + 32 * B + 16)[ly])

        @block.gpsimd
        def _(pool):
            pool.memset(v_head[:, :, :, :], 1.0).then_inc(pool_step, 1)
            pool.memset(zeros[:, :], 0.0).then_inc(pool_step, 1)
            pool.wait_ge(pool_step, 2)
            steps = 2
            per_group = 3

            def copy_v_head(slot, h):
                pool.sem_inc(passed, 1)
                pool.tensor_copy(v_head[:, slot, :, 0:DH], v_all[:, :, bass.ds(DH * h, DH)])\
                    .then_inc(v_head_ready, 1)

            def split_max(ly, hb, h, g):
                cols = (slice(TT // 2, TT), slice(0, TT // 2))[g]
                pool.wait_ge(m_ready, upto(2, ly, hb, h, g + 1))
                pool.sem_inc(passed, 1)
                pool.tensor_copy(cpart[:, g, 0, :], negmax[:, cols]).then_inc(pool_step, 1)
                pool.wait_ge(pool_step, upto(2 * per_group, ly, hb, h, steps + g * per_group + 1))
                pool.tensor_tensor(cres[:, g, :], negmax[:, cols], cpart[:, g, 0, :], ALU.subtract)\
                    .then_inc(pool_step, 1)
                pool.wait_ge(pool_step, upto(2 * per_group, ly, hb, h, steps + g * per_group + 2))
                pool.sem_inc(passed, 1)
                pool.tensor_copy(cpart[:, g, 1, :], cres[:, g, :]).then_inc(pool_step, 1)
                pool.wait_ge(pool_step, upto(2 * per_group, ly, hb, h, steps + g * per_group + 3))
                pool.tensor_tensor(cpart[:, g, 2, :], cres[:, g, :], cpart[:, g, 1, :], ALU.subtract)\
                    .then_inc(c_ready, 1)

            for ly in range(2):
                with pool.Fori(0, B) as b:
                    b16 = b * TT
                    if ly:
                        for u in range(4 * NQ):
                            pool.wait_ge(rotated, b16 + (u + 1))
                            pool.tensor_tensor(qf[:, u % 2, :], rot1[:, u % 2, :], rot2[:, u % 2, :], ALU.add)\
                                .then_inc(roped, 1)
                    pool.wait_ge(v_ready, upto(1, ly, b16, TT))
                    copy_v_head(0, 0)
                    split_max(ly, b16, 0, 0)
                    split_max(ly, b16, 0, 1)
                    with pool.Fori(0, (H - 2) // 2) as i:
                        hb = b16 + 2 * i
                        for j in range(2):
                            split_max(ly, hb, j + 1, 0)
                            split_max(ly, hb, j + 1, 1)
                            copy_v_head((j + 1) % 2, 2 * i + j + 1)
                    split_max(ly, b16, H - 1, 0)
                    split_max(ly, b16, H - 1, 1)
                    copy_v_head((H - 1) % 2, H - 1)
                    for t in range(TT):
                        pool.wait_ge(y_added, upto(1, ly, b16, t + 1))
                        if ly == 0:
                            pool.tensor_tensor(xb[:, t, :], xb[:, t, :], bo_bc[:, :], ALU.add).then_inc(x_ready, 1)
                        else:
                            half, col = t // 8, (t % 8) * D
                            pool.tensor_tensor(xT[:, half, col:col + D], xb[:, t, :], fb_bc[:, :], ALU.add)\
                                .then_inc(x_ready, 1)
                for t in range(NFT):
                    pool.wait_ge(fy_added, (ly + 1) * E * NFT)
                    pool.tensor_tensor(xb[:, t, :], xb[:, t, :], facc[:, t, :], ALU.add)\
                        .then_inc(pool_step if ly else x_ready, 1)
                if ly:
                    done = steps + 2 * 2 * B * H * per_group
                    for t in range(NFT):
                        pool.wait_ge(pool_step, done + t + 1)
                        pool.tensor_tensor(xb[:, t, :], xb[:, t, :], fb_bc[:, :], ALU.add).then_inc(x_ready, 1)

        @block.scalar
        def _(act):
            def turn_out(ly, b16, n):
                for t in range(n):
                    act.wait_ge(xn_turned, ln_tile(ly, b16, t + 1))
                    act.activation(xT[:, :, t * P:(t + 1) * P],
                                   ps_m[:, t % 2, 0:D].rearrange("p (k n) -> p k n", k=KD), ACT.Copy)\
                        .then_inc(xT_ready, 1)

            def std(n, norm):
                act.wait_ge(var_ready, norm + 1)
                act.activation(sd[:, 0:n], vpe[:, 0:n], ACT.Sqrt).then_inc(sd_ready, 1)

            def acc_evac(ly, hb, h, qt):
                act.wait_ge(pv_mm, upto(10, ly, hb, h, {3: 4, 2: 7, 1: 9, 0: 10}[qt]))
                if qt < NQ - 2:
                    act.wait_ge(o_mm, upto(NQ, ly, hb, h, NQ - 2 - qt))
                act.activation(acc_sb[:, qt % 2, :], ps_acc[:, :], ACT.Copy).then_inc(acc_out, 1)

            def exps(ly, hb, h, first, last):
                for n, (qt, c, blocks) in enumerate(CHUNK):
                    w = sum(x[2] for x in blocks)
                    act.wait_ge(s_mm, upto(CHUNKS, ly, hb, h, n + 1))
                    if n >= 4 or not first:
                        act.wait_ge(pv_mm, upto(10, ly, hb, h, n // 2 - 1))
                    act.activation(probs[:, n % 4, 0:w], ps_s[:, n % 2, 0:w], ACT.Exp).then_inc(exp_done, 1)
                    if n == 1 and not first:
                        acc_evac(ly, hb, h - 1, 0)
                    if n % 2 and (n - 3) // 2 in (3, 6, 8):
                        acc_evac(ly, hb, h, LAST_GROUP[(n - 3) // 2])
                if last:
                    acc_evac(ly, hb, h, 0)

            act.wait_ge(consts_in, CONSTS)
            act.activation(bqk[:, 0, :], bqk[:, 0, :], ACT.Copy, scale=DH ** -0.5).then_inc(bq_scaled, 1)
            act.wait_ge(bq_scaled, 1)
            for ly in range(2):
                with act.Fori(0, B) as b:
                    b16 = b * TT
                    std(TT, b + ly * (B + 1))
                    turn_out(ly, b16, TT)
                    if ly:
                        for t in range(TT):
                            act.wait_ge(v_mm, upto(1, ly, b16, t + 1))
                            act.activation(v_all[:, t, :], ring[:, t % 4, 0:D], ACT.Copy).then_inc(v_ready, 1)
                    for u in range(4 * NQ):
                        half, proj, n = u // 8, u // 4 % 2, u % 4
                        first = part(proj, half, 0)[:, n * QW:(n + 1) * QW]
                        if ly == 0:
                            act.wait_ge(qk_mm, upto(1, ly, b16, u + 1))
                            if u >= 2:
                                act.wait_ge(qk_split, upto(1, ly, b16, u - 1))
                            sc, bias = (DH ** -0.5, 1.0)[proj], bqk[:, proj, half:half + 1]
                            act.activation(qf[:, u % 2, :], ring[:, u % 4, :], ACT.Identity, bias=bias, scale=sc)
                            act.activation(first, ring[:, u % 4, :], ACT.Identity, bias=bias, scale=sc)\
                                .then_inc(qk_out, 1)
                        else:
                            act.wait_ge(roped, b16 + (u + 1))
                            act.activation(first, qf[:, u % 2, :], ACT.Copy).then_inc(qk_out, 1)
                    with act.Fori(0, H // GROUP - 1) as i:
                        hb = b16 + GROUP * i
                        for j in range(GROUP):
                            exps(ly, hb, j, j == 0, j == GROUP - 1)
                    for j in range(GROUP):
                        exps(ly, b16, H - GROUP + j, j == 0, j == GROUP - 1)
                    for t in range(TT):
                        act.wait_ge(ot_mm, upto(1, ly, b16, t + 1))
                        if t >= 2:
                            act.wait_ge(y_mm, upto(1, ly, b16, t - 1))
                        act.activation(o_t[:, t % 2, :], ps_m[:, t % 2, 0:D], ACT.Copy).then_inc(ot_out, 1)
                std(NFT, ly * (B + 1) + B)
                turn_out(ly, B * TT, NFT)
                with act.Fori(0, E // 2) as ep:
                    for s in range(2):
                        for n in range(2):
                            step = ep * 4 + (ly * E * 2 + 2 * s + n)
                            act.wait_ge(fy_mm, step * 4 + NFT + 1 - 4)
                            for f in range(NF):
                                act.wait_ge(h_mm, step * NF + f + 1)
                                act.activation(hid[:, n, f, :], ring[:, f % 4, :], ACT.Gelu).then_inc(gelu_out, 1)

        @block.tensor
        def _(pe):
            pe.wait_ge(consts_in, CONSTS)
            pe.wait_ge(pool_step, 2)
            pe.sem_inc(stack_free, SLOTS)
            pe.sem_inc(o_norm, 1)

            def turn_xn(ly, b16, n):
                for t in range(n):
                    pe.wait_ge(xn_ready, ln_tile(ly, b16, t + 1))
                    if t >= 2:
                        pe.wait_ge(xT_ready, ln_tile(ly, b16, t - 1))
                    for k in range(KD):
                        mm = pe.transpose(ps_m[:, t % 2, k * P:(k + 1) * P], xn[:, t % 4, k * P:(k + 1) * P],
                                          identf[:, :])
                    mm.then_inc(xn_turned, 1)

            def project_v(ly, b16):
                at = (2 * D, 2 * D)[ly]
                for t in range(TT):
                    pe.wait_ge(xT_ready, ln_tile(ly, b16, t + 1))
                    if t >= 4:
                        pe.wait_ge(v_ready, upto(1, ly, b16, t - 3))
                    for k in range(KD):
                        mm = pe.matmul(ring[:, t % 4, 0:D], xT[:, k, t * P:(t + 1) * P], wqkv[:, k, at:at + D],
                                       start=(k == 0), stop=(k == KD - 1))
                    mm.then_inc(v_mm, 1)
                pe.wait_ge(v_ready, upto(1, ly, b16, TT))

            def project_qk(ly, b16):
                for u in range(4 * NQ):
                    half, proj, n = u // 8, u // 4 % 2, u % 4
                    if ly == 0:
                        if u >= 4:
                            pe.wait_ge(qk_out, upto(1, ly, b16, u - 3))
                        outs = ((u % 4, proj * D),)
                    else:
                        if u >= 2:
                            pe.wait_ge(rotated, b16 + (u - 1))
                        outs = ((2 * (u % 2), proj * D), (2 * (u % 2) + 1, (3 + proj) * D))
                    for bank, at in outs:
                        at += half * P
                        for k in range(KD):
                            mm = pe.matmul(ring[:, bank, :], wqkv[:, k, at:at + P], xT[:, k, n * QW:(n + 1) * QW],
                                           start=(k == 0), stop=(k == KD - 1))
                    mm.then_inc(qk_mm, 1)

            def item(ly, hb, h, at, what, slot):
                before = item_count(ly, hb, h, at)
                bank = (len(FIRST_STREAM) * (h is not None) + at) % 2
                nxt = 0 if h is None else h + 1
                if what in (LO, HI):
                    g, of = (1, h) if what == LO else (0, nxt)
                    pe.wait_ge(c_ready, upto(2, ly, hb, of, g + 1))
                if h is not None or at >= 2:
                    pe.wait_ge(item_used, before - 1)
                if what in (LO, HI):
                    pe.transpose(c_ps[bank][0:3 * TT // 2, :], cpart[:, g, :, :].rearrange("p i t -> p (i t)"),
                                 identb[:, :]).then_inc(item_mm, 1)
                    return
                qb, kc, w = UNIT[what]
                rows = c_row[ly]
                if what == 0:
                    pe.wait_ge(stack_in[slot], stack_count(ly, hb, nxt, slot))
                mm = pe.matmul(ps_m[:, bank, 0:w], q_stack(slot)[0:rows, qb * P:(qb + 1) * P],
                               k_stack(slot)[0:rows, kc * QW:kc * QW + w], start=True, stop=True)
                if kc == qb // 4:
                    mm = pe.matmul(ps_m[:, bank, w - P:w], identb[:, :], masks[:, 0, :], start=False, stop=True,
                                   skip_group_check=True)
                mm.then_inc(item_mm, 1)

            def stack_count(ly, hb, h, slot):
                per_a, per_b = 16 * (LOADS + 2), 16 * LOADS
                per = (per_a, per_b)[ly]
                before = per_a * B * (H // SLOTS) if ly else 0
                return hb * (per // SLOTS) + (before + per // SLOTS * (h - slot) + per)

            def rows_count(ly, hb, h, slot):
                per = 16 * 3
                return hb * (per // SLOTS) + per // SLOTS * (ly * B * H + h - slot + SLOTS)

            def scores(ly, hb, h, n, slot, first):
                qt, c, blocks = CHUNK[n]
                rows = c_row[ly] + 3
                if n == 0:
                    pe.wait_ge(rows_in[0][slot], rows_count(ly, hb, h, slot))
                if qt == 1 and c == 0:
                    pe.wait_ge(rows_in[1][slot], rows_count(ly, hb, h, slot))
                if n >= 2 or not first:
                    pe.wait_ge(exp_done, upto(CHUNKS, ly, hb, h, n - 1))
                for kb, q0, w, at in blocks:
                    to = ps_s[:, n % 2, at:at + w]
                    diagonal = kb >= 4 * qt
                    mm = pe.matmul(to, k_stack(slot)[0:rows, kb * P:(kb + 1) * P],
                                   q_stack(slot)[0:rows, qt * QW + q0:(qt + 1) * QW], start=True, stop=True)
                    if diagonal:
                        mm = pe.matmul(to[:, 0:P], identb[:, :], masks[:, 1, :], start=False, stop=True,
                                       skip_group_check=True)
                mm.then_inc(s_mm, 1)

            def times_v(ly, hb, h, g, slot2):
                pe.wait_ge(exp_done, upto(CHUNKS, ly, hb, h, 2 * g + 2))
                if g == 0:
                    pe.wait_ge(v_head_ready, upto(1, ly, hb, h, 1))
                fresh = g in FIRST_GROUP
                if g == 9:
                    mm = pe.matmul(ps_acc[:, :], zeros[:, 0:P], zeros[:, :], start=True, stop=False,
                                   skip_group_check=True)
                    mm.then_inc(stack_free, 1)
                    fresh = False
                r = 0
                for n in (2 * g, 2 * g + 1):
                    qt, _, blocks = CHUNK[n]
                    for kb, q0, w, at in blocks:
                        mm = pe.matmul(ps_acc[32 * r:32 * r + 32, q0:QW], v_head[:, slot2, kb, :],
                                       probs[:, n % 4, at:at + w], start=fresh, stop=g in LAST_GROUP,
                                       skip_group_check=True)
                        r += 1
                mm.then_inc(pv_mm, 1)

            def outputs(ly, hb, h, qt):
                pe.wait_ge(acc_out, upto(NQ, ly, hb, h, NQ - qt))
                if qt == NQ - 1:
                    pe.wait_ge(o_norm, upto(1, ly, hb, h, 1))
                for c in range(4):
                    mm = pe.matmul(o_ps[:, 4 * qt + c, :], acc_sb[:, qt % 2, c * P:(c + 1) * P], sel[:, :],
                                   start=True, stop=True)
                mm.then_inc(o_mm, 1)

            def attend(ly, hb, h, slot, first, last, more):
                at = 0
                for n, items in enumerate(stream(more)):
                    scores(ly, hb, h, n, slot, first)
                    for what in items:
                        item(ly, hb, h, at, what, (slot + 1) % SLOTS)
                        at += 1
                    if n == 1 and not first:
                        outputs(ly, hb, h - 1, 1)
                        times_v(ly, hb, h - 1, 9, (slot - 1) % 2)
                    if n == 3 and not first:
                        outputs(ly, hb, h - 1, 0)
                    if n % 2 and n >= 3:
                        g = (n - 3) // 2
                        if g in (4, 7):
                            outputs(ly, hb, h, FIRST_GROUP[g] + 1)
                        times_v(ly, hb, h, g, slot % 2)
                if last:
                    outputs(ly, hb, h, 1)
                    times_v(ly, hb, h, 9, slot % 2)
                    outputs(ly, hb, h, 0)

            for ly in range(2):
                pe.wait_ge(weights_in, 32 * (ly + 1))
                pe.wait_ge(ones_in, 16 * SLOTS * (ly + 1))
                with pe.Fori(0, B) as b:
                    b16 = b * TT
                    turn_xn(ly, b16, TT)
                    project_v(ly, b16)
                    project_qk(ly, b16)
                    for at, what in enumerate(FIRST_STREAM):
                        item(ly, b16, None, at, what, 0)
                    with pe.Fori(0, H // GROUP - 1) as i:
                        hb = b16 + GROUP * i
                        for j in range(GROUP):
                            attend(ly, hb, j, j, j == 0, j == GROUP - 1, True)
                    for j in range(GROUP):
                        attend(ly, b16, H - GROUP + j, j, j == 0, j == GROUP - 1, j < GROUP - 1)
                    pe.wait_ge(o_norm, upto(1, ly, b16, H, 1))
                    for t in range(TT + 1):
                        if t < TT:
                            if t >= 2:
                                pe.wait_ge(ot_out, upto(1, ly, b16, t - 1))
                            for k in range(KD):
                                mm = pe.transpose(ps_m[:, t % 2, k * P:(k + 1) * P], oh[:, t, k * P:(k + 1) * P],
                                                  identf[:, :])
                            mm.then_inc(ot_mm, 1)
                        if t >= 1:
                            pe.wait_ge(ot_out, upto(1, ly, b16, t))
                            if t - 1 >= 4:
                                pe.wait_ge(y_added, upto(1, ly, b16, t - 4))
                            for k in range(KD):
                                mm = pe.matmul(ring[:, (t - 1) % 4, 0:D], o_t[:, (t - 1) % 2, k * P:(k + 1) * P],
                                               wo[:, k, :], start=(k == 0), stop=(k == KD - 1))
                            mm.then_inc(y_mm, 1)
                    pe.wait_ge(y_added, upto(1, ly, b16, TT))
                turn_xn(ly, B * TT, NFT)
                pe.wait_ge(xT_ready, ln_tile(ly, B * TT, NFT))
                if ly == 0:
                    pe.sem_inc(fy_mm, NFT + 1)
                with pe.Fori(0, E // 2) as ep:
                    for s in range(2):
                        pe.wait_ge(ew_in[s], 32 * (ly * (E // 2) + ep + 1))
                        for n in range(2):
                            step = ep * 4 + (ly * E * 2 + 2 * s + n)
                            for f in range(NF):
                                if f >= 4:
                                    pe.wait_ge(gelu_out, step * NF + f - 3)
                                for k in range(KD):
                                    mm = pe.matmul(ring[:, f % 4, :], w1_sb[:, s, k, f * P:(f + 1) * P],
                                                   xT[:, k, n * QW:(n + 1) * QW], start=(k == 0), stop=(k == KD - 1))
                                mm.then_inc(h_mm, 1)
                            pe.wait_ge(gelu_out, step * NF + NF)
                            for t in range(4):
                                if t >= 2:
                                    pe.wait_ge(fy_added, step * 4 + t - 1)
                                for f in range(NF):
                                    mm = pe.matmul(ps_m[:, t % 2, 0:D], hid[:, n, f, t * P:(t + 1) * P],
                                                   w2_sb[:, s, f, :], start=(f == 0), stop=(f == NF - 1))
                                mm.then_inc(fy_mm, 1)
                            pe.wait_ge(fy_added, step * 4 + 4)

        @block.vector
        def _(dve):
            dve.memset(part_max[:, :, :], LOWEST).then_inc(dve_step, 1)
            dve.wait_ge(consts_in, CONSTS)
            dve.tensor_copy(eixf[:, :, :], eix[:, :, :]).then_inc(dve_step, 1)
            dve.wait_ge(dve_step, 2)
            for e in range(E):
                dve.scalar_tensor_tensor(out=epick[:, e, :, :], in0=eixf[:, :, :], scalar=float(e), in1=ewt[:, :, :],
                                         op0=ALU.is_equal, op1=ALU.mult).then_inc(dve_step, 1)
            dve.wait_ge(dve_step, 2 + E)
            dve.tensor_tensor(wtok[:, :, :], epick[:, :, :, 0], epick[:, :, :, 1], ALU.add).then_inc(dve_step, 1)
            dve.wait_ge(dve_step, 3 + E)
            base0 = 3 + E

            ln_steps = 7
            step_batch = (ln_steps + 2 * 4 * NQ + H, ln_steps + 1 + 2 * 4 * NQ + H)
            step_layer = B * step_batch[0] + ln_steps

            def norm(ly, b16, nth, n, base, bias):
                def before(k):
                    return base_all(k - 1)

                base_all = base
                dve.wait_ge(x_in_sb, 16 * (nth + 1))
                if bias:
                    for t in range(n):
                        mm = dve.tensor_tensor(xb[:, t, :], xb[:, t, :], fb_bc[:, :], ALU.add)
                    mm.then_inc(dve_step, 1)
                    dve.wait_ge(dve_step, base(1))
                else:
                    base = before
                for t in range(n):
                    mm = dve.bn_stats(stats[:, t, :], xb[:, t, :])
                mm.then_inc(dve_step, 1)
                dve.wait_ge(dve_step, base(2))
                dve.sem_inc(passed, 1)
                for t in range(n):
                    mm = dve.bn_aggr(mv[:, t, :], stats[:, t, :])
                mm.then_inc(dve_step, 1)
                dve.wait_ge(dve_step, base(3))
                dve.tensor_scalar_add(vpe[:, 0:n], mv[:, 0:n, 1], EPS).then_inc(var_ready, 1)
                dve.wait_ge(sd_ready, nth + 1)
                dve.reciprocal(r0[:, 0:n], sd[:, 0:n]).then_inc(dve_step, 1)
                dve.wait_ge(dve_step, base(4))
                dve.tensor_tensor(r1[:, 0:n], r0[:, 0:n], r0[:, 0:n], ALU.mult).then_inc(dve_step, 1)
                dve.wait_ge(dve_step, base(5))
                dve.tensor_tensor(r1[:, 0:n], r1[:, 0:n], vpe[:, 0:n], ALU.mult).then_inc(dve_step, 1)
                dve.wait_ge(dve_step, base(6))
                dve.tensor_scalar(r1[:, 0:n], r1[:, 0:n], -0.5, 1.5, ALU.mult, ALU.add).then_inc(dve_step, 1)
                dve.wait_ge(dve_step, base(7))
                dve.tensor_tensor(rstd[:, 0:n], r0[:, 0:n], r1[:, 0:n], ALU.mult).then_inc(dve_step, 1)
                dve.wait_ge(dve_step, base(8))
                for t in range(n):
                    if t >= 4:
                        dve.wait_ge(xn_turned, ln_tile(ly, b16, t - 3))
                    dve.tensor_scalar(xn[:, t % 4, :], xb[:, t, :], mv[:, t, 0:1], rstd[:, t:t + 1],
                                      ALU.subtract, ALU.mult).then_inc(xn_ready, 1)

            def use_item(ly, hb, h, at, what):
                before = item_count(ly, hb, h, at)
                bank = (len(FIRST_STREAM) * (h is not None) + at) % 2
                dve.wait_ge(item_mm, before + 1)
                if what in (LO, HI):
                    g = (1, 0)[what == HI]
                    dve.tensor_copy(crow[:, g, :], c_ps[bank][0:3 * TT // 2, :]).then_inc(item_used, 1)
                    return
                qb, kc, w = UNIT[what]
                dve.reduce_max(part_max[:, qb, kc:kc + 1], ps_m[:, bank, 0:w], AX_X).then_inc(item_used, 1)
                if what + 1 in (HI_UNITS, UNITS):
                    g = (HI_UNITS, UNITS).index(what + 1)
                    cols = (slice(TT // 2, TT), slice(0, TT // 2))[g]
                    dve.wait_ge(item_used, before + 1)
                    dve.tensor_reduce(negmax[:, cols], part_max[:, cols, :], AX_X, ALU.max, negate=True)\
                        .then_inc(m_ready, 1)

            def beside(ly, hb, h, more, col, step):
                at = 0
                for n, items in enumerate(stream(more)):
                    for what in items:
                        use_item(ly, hb, h, at, what)
                        at += 1
                    if n == 4 and step is not None:
                        normalise(ly, hb, h - 1, col, step)

            def normalise(ly, hb, h, col, base):
                dve.wait_ge(o_mm, upto(NQ, ly, hb, h, NQ))
                dve.reciprocal(recip[:, :], o_ps[:, :, DH]).then_inc(dve_step, 1)
                dve.wait_ge(dve_step, base(1))
                dve.tensor_tensor(oh[:, :, bass.ds(col, DH)], o_ps[:, :, 0:DH],
                                  recip[:, :].rearrange("p (t o) -> p t o", o=1).broadcast_to([P, TT, DH]), ALU.mult)\
                    .then_inc(o_norm, 1)

            def rotate(b16, u):
                proj, n = u // 4 % 2, u % 4
                cols = slice(n * QW, (n + 1) * QW)
                dve.wait_ge(qk_mm, upto(1, 1, b16, u + 1))
                if u >= 2:
                    dve.wait_ge(roped, b16 + (u - 1))
                sc = (DH ** -0.5, 1.0)[proj]
                dve.scalar_tensor_tensor(out=rot1[:, u % 2, :], in0=ring[:, 2 * (u % 2), :], scalar=sc,
                                         in1=cosb[:, cols], op0=ALU.mult, op1=ALU.mult)
                dve.scalar_tensor_tensor(out=rot2[:, u % 2, :], in0=ring[:, 2 * (u % 2) + 1, :], scalar=sc,
                                         in1=sinb[:, cols], op0=ALU.mult, op1=ALU.mult).then_inc(rotated, 1)

            def split(ly, b16, u, at):
                half, proj, n = u // 8, u // 4 % 2, u % 4
                p1, p2, p3 = (part(proj, half, i)[:, n * QW:(n + 1) * QW] for i in range(3))
                dve.wait_ge(qk_out, upto(1, ly, b16, u + 1))
                dve.tensor_tensor(res[:, u % 2, :], qf[:, u % 2, :], p1, ALU.subtract).then_inc(dve_step, 1)
                dve.wait_ge(dve_step, at(2 * u + 1))
                dve.tensor_copy(p2, res[:, u % 2, :]).then_inc(dve_step, 1)
                dve.wait_ge(dve_step, at(2 * u + 2))
                dve.tensor_tensor(p3, res[:, u % 2, :], p2, ALU.subtract).then_inc(qk_split, 1)

            for ly in range(2):
                with dve.Fori(0, B) as b:
                    b16 = b * TT

                    def base(k):
                        return b * step_batch[ly] + (base0 + ly * step_layer + k)

                    def at(k):
                        return base(ln_steps + ly + k)

                    norm(ly, b16, b + ly * (B + 1), TT, base, ly == 1)
                    if ly == 0:
                        for t in range(TT):
                            dve.wait_ge(v_mm, upto(1, ly, b16, t + 1))
                            dve.tensor_tensor(v_all[:, t, :], ring[:, t % 4, 0:D], bv_bc[:, :], ALU.add)\
                                .then_inc(v_ready, 1)
                    if ly:
                        rotate(b16, 0)
                    for u in range(4 * NQ):
                        if ly and u + 1 < 4 * NQ:
                            rotate(b16, u + 1)
                        split(ly, b16, u, at)

                    for i, what in enumerate(FIRST_STREAM):
                        use_item(ly, b16, None, i, what)
                    with dve.Fori(0, H // GROUP - 1) as i:
                        hb = b16 + GROUP * i

                        def step(j):
                            return lambda k: GROUP * i + at(2 * 4 * NQ + j + k)

                        for j in range(GROUP):
                            beside(ly, hb, j, True, DH * GROUP * i + DH * (j - 1), step(j - 1) if j else None)
                        j = GROUP - 1
                        normalise(ly, hb, j, DH * GROUP * i + DH * j, step(j))
                    for h in range(H - GROUP, H):

                        def step(h):
                            return lambda k: at(2 * 4 * NQ + h + k)

                        beside(ly, b16, h, h < H - 1, DH * (h - 1), step(h - 1) if h > H - GROUP else None)
                    normalise(ly, b16, H - 1, DH * (H - 1), step(H - 1))
                    for t in range(TT):
                        dve.wait_ge(y_mm, upto(1, ly, b16, t + 1))
                        dve.tensor_tensor(xb[:, t, :], xb[:, t, :], ring[:, t % 4, 0:D], ALU.add)\
                            .then_inc(y_added, 1)

                def base(k):
                    return base0 + ly * step_layer + B * step_batch[ly] + k

                norm(ly, B * TT, ly * (B + 1) + B, NFT, base, False)
                dve.memset(facc, 0.0).then_inc(facc_zero, 1)
                dve.wait_ge(facc_zero, ly + 1)
                with dve.Fori(0, E // 2) as ep:
                    for s in range(2):
                        for n in range(2):
                            step = ep * 4 + (ly * E * 2 + 2 * s + n)
                            for t in range(4):
                                tile = 4 * n + t
                                dve.wait_ge(fy_mm, step * 4 + t + NFT + 2)
                                dve.scalar_tensor_tensor(out=facc[:, tile, :], in0=ps_m[:, t % 2, 0:D],
                                                         scalar=wtok[:, bass.ds(2 * ep + s, 1), tile],
                                                         in1=facc[:, tile, :], op0=ALU.mult, op1=ALU.add)\
                                    .then_inc(fy_added, 1)


def kernel(**inputs):
    import ml_dtypes
    import concourse.bacc as bacc
    from concourse.bass_utils import run_bass_kernel_spmd as run

    bf = ml_dtypes.bfloat16
    g = {k: np.asarray(v) for k, v in inputs.items()}
    x = g["L0_attn_a_x"].reshape(B * L, D)
    w_a = np.concatenate([g["L0_attn_a_Wq"].T, g["L0_attn_a_Wk"].T, g["L0_attn_a_Wv"].T], axis=1)
    kqv = g["L0_attn_b_W_KQV"]
    wk, wq, wv = kqv[0:D], kqv[D:2 * D], kqv[2 * D:]
    swap = np.arange(D) ^ 1
    w_b = np.concatenate([wq.T, wk.T, wv.T, wq[swap].T, wk[swap].T], axis=1)
    bqk = np.stack([g["L0_attn_a_bq"].reshape(KD, P).T, g["L0_attn_a_bk"].reshape(KD, P).T], axis=1)

    pos = np.arange(L)
    inv = (1.0 / np.float32(10000.0) ** (np.arange(0, DH, 2, dtype=np.float32) / np.float32(DH))).astype(np.float32)
    freqs = (pos.astype(np.float32)[:, None] * inv[None, :]).astype(np.float32)
    feat = np.arange(P) % DH
    cos_t = np.cos(freqs).astype(np.float32)[:, feat // 2].T
    sin_t = (np.sin(freqs).astype(np.float32)[:, feat // 2] * np.where(feat % 2, 1, -1)).T.astype(np.float32)
    slopes = np.power(np.float32(2.0), (np.float32(-8.0) * np.arange(1, H + 1, dtype=np.float32) / np.float32(H)))
    slopes = slopes.astype(np.float32)
    cut, rest = [], slopes.copy()
    for _ in range(3):
        s = rest.astype(bf)
        cut.append(s.astype(np.float32))
        rest = (rest - cut[-1]).astype(np.float32)
    q_pos = np.zeros((H, POS, L), np.float32)
    k_pos = np.zeros((H, POS, L), np.float32)
    for i in range(3):
        for u, p in enumerate((pos // P * P, pos % P)):
            q_pos[:, 4 * i + 2 * u] = p
            k_pos[:, 4 * i + 2 * u] = -cut[i][:, None]
            q_pos[:, 4 * i + 2 * u + 1] = cut[i][:, None]
            k_pos[:, 4 * i + 2 * u + 1] = p
    eye = np.eye(P, dtype=np.float32)
    r, c = np.arange(P)[:, None], np.arange(P)[None, :]
    mask = np.stack([np.where(c > r, MASKED, 0.0), np.where(r > c, MASKED, 0.0)], axis=1)
    sel = np.zeros((P, DH + 1), np.float32)
    for q in range(4):
        for d in range(DH + 1):
            sel[32 * q + d, d] = 1.0

    def rows(v):
        return np.ascontiguousarray(np.broadcast_to(v[None, :], (P, D)))

    arrays = {
        "x_in": x, "w_a": w_a, "wo_a": g["L0_attn_a_Wo"].T, "bqk_a": bqk, "bv_a": rows(g["L0_attn_a_bv"]),
        "bo_a": rows(g["L0_attn_a_bo"]), "w_b": w_b, "wo_b": g["L0_attn_b_W_O"].T, "cos_t": cos_t, "sin_t": sin_t,
        "q_pos": q_pos.astype(bf), "k_pos": k_pos.astype(bf), "ones_rows": np.ones((3, L), bf),
        "ident_f": eye, "ident_b": eye.astype(bf), "mask_in": mask.astype(bf), "sel_in": sel,
        "e_w": g["L0_ffn_expert_weights"], "e_idx": g["L0_ffn_expert_indices"],
        "w1": g["L0_ffn_w1"], "w2": g["L0_ffn_w2"], "fbias": rows(g["L0_ffn_bias"]),
    }
    nc = bacc.Bacc("TRN2", target_bir_lowering=False, num_devices=1)
    aps, maps = {}, {}
    for name, a in arrays.items():
        a = np.ascontiguousarray(a)
        maps[name + "_dram"] = a
        aps[name] = nc.dram_tensor(name + "_dram", a.shape, mybir.dt.from_np(a.dtype), kind="ExternalInput").ap()
    aps["ident_in"] = (aps.pop("ident_f"), aps.pop("ident_b"))
    aps["out"] = nc.dram_tensor("out_dram", (B * L, D), F32, kind="ExternalOutput").ap()
    build(nc, **aps)
    res = run(nc, [maps], core_ids=[0])
    return res.results[0]["out_dram"].reshape(B, L, D)
```

```python
from contextlib import ExitStack

import numpy as np

import concourse.bass as bass
from concourse import mybir

F32 = mybir.dt.float32
BF16 = mybir.dt.bfloat16
I32 = mybir.dt.int32
ALU = mybir.AluOpType
ACT = mybir.ActivationFunctionType
AX_X = mybir.AxisListType.X

P = 128
B, L, D = 4, 2048, 256
H, DH = 16, 16
KD = D // P
TT = L // P
QW = 512
NQ = L // QW
E, FF, TOPK = 8, 1024, 2
FT = 1024
NFT = FT // P
NF = FF // P
ROUTED = 2
EPS = 1e-5
MASKED = -1e30
LOWEST = -3.0e38

SLOTS = 4
GROUP = 4
NPART = 6
Q_PARTS = (0, 0, 0, 1, 1, 2)
K_PARTS = (0, 1, 2, 0, 1, 0)
POS = 12

UNITS = sum(4 * (qt + 1) for qt in range(NQ))
BLOCKS = sum(4 * (qt + 1) for qt in range(NQ))
LOADS = 2 * NPART
CONSTS = 16 * 13

BLOCK = [(qt, kb, max(0, P * (kb - 4 * qt))) for qt in reversed(range(NQ)) for kb in range(4 * qt + 4)]
UNIT = [(qb, kc, QW if kc < qt else P * (qb - 4 * qt + 1))
        for qt in reversed(range(NQ)) for qb in range(4 * qt, 4 * qt + 4) for kc in range(qt + 1)]
HI_UNITS = sum(1 for qb, _, _ in UNIT if qb >= TT // 2)
LO, HI = -1, -2
LO_STEP, HI_STEP = 5, 32
FIRST_LO = next(n for n, x in enumerate(BLOCK) if x[0] == 1)


def stream(with_next):
    return [([n] if with_next else []) + ([LO] if n == LO_STEP else []) +
            ([HI] if with_next and n == HI_STEP else []) for n in range(BLOCKS)]


FIRST_HI = 36
FIRST_STREAM = list(range(FIRST_HI)) + [HI] + list(range(FIRST_HI, UNITS))
ITEMS = UNITS + 2
MBANKS = 3
assert ITEMS % MBANKS == 0
LAST_GROUP = {3: 3, 6: 2, 8: 1, 9: 0}
FIRST_GROUP = {0: 3, 4: 2, 7: 1, 9: 0}
GROUPS = BLOCKS // 4

ROT = 8
PV_LAG = 6
SUM_STEP, TURN_STEP = 5, 7
ACC_STEP = {19: 3, 31: 2, 39: 1}


def steps_of(h):
    return [(0, n) for n in range(ROT, BLOCKS)] + [(1, n) for n in range(ROT)]


def projections():
    seq = [("q", u) for u in range(2 * NQ)] + [("v", t) for t in range(TT // 2)]
    rest = [x for i in range(TT // 2) for x in (("v", TT // 2 + i), ("q", 2 * NQ + i))]
    done = 0
    for i, x in enumerate(rest):
        seq.append(x)
        while done < len(FIRST_STREAM) * (i + 1) // len(rest):
            seq.append(("m", done))
            done += 1
    return seq


PROJECTIONS = projections()
JOBS = [x for x in PROJECTIONS if x[0] != "m"]


def build(nc, x_in, w_a, wo_a, bqk_a, bv_a, bo_a, w_b, wo_b, cos_t, sin_t, q_pos, k_pos, ones_rows,
          ident_in, mask_in, sel_in, e_w, e_idx, w1, w2, fbias, out):
    x_a = nc.dram_tensor("x_after_a", (B * L, D), F32, kind="Internal").ap()
    x_raw = nc.dram_tensor("x_before_ffn", (B * FT, D), F32, kind="Internal").ap()

    with ExitStack() as ctx:
        def sb(name, shape, dt=F32):
            return ctx.enter_context(nc.sbuf_tensor(name, shape, dt))

        def sem(name):
            return ctx.enter_context(nc.semaphore(name))

        xb = sb("xb", [P, TT, D])
        xn = sb("xn", [P, TT, D])
        xT_f = sb("xT", [P, KD * L])
        parts_f = sb("parts", [P, 12 * L // 2])
        stack_f = sb("stacks", [P, 2 * SLOTS * L // 2])
        v_all = sb("v_all", [P, TT, D])
        v_head = sb("v_head", [P, 2, TT, 2 * DH])
        probs = sb("probs", [P, 8, QW])
        acc_sb = sb("acc_sb", [P, NQ, QW])
        osum = sb("osum", [P, QW])
        wqkv = sb("wqkv", [P, KD, 5 * D])
        wo = sb("wo", [P, KD, D])
        cosb = sb("cosb", [P, L])
        sinb = sb("sinb", [P, L])
        fb_bc = sb("fb_bc", [P, D])
        bqk = sb("bqk", [P, 2, KD])
        identf = sb("identf", [P, P])
        identb = sb("identb", [P, P], BF16)
        mask = sb("mask", [P, QW], BF16)
        early = sb("early", [P, P], BF16)
        sel = sb("sel", [P, 2 * DH])
        zeros = sb("zeros", [P, P], BF16)
        stats = sb("stats", [P, TT, 6])
        mv = sb("mv", [P, TT, 2])
        vpe = sb("vpe", [P, TT])
        sd = sb("sd", [P, TT])
        r0 = sb("r0", [P, TT])
        r1 = sb("r1", [P, TT])
        rstd = sb("rstd", [P, TT])
        part_max = sb("part_max", [P, TT, NQ])
        negmax = sb("negmax", [P, TT])
        cres = sb("cres", [P, 2, TT // 2])
        cpart = sb("cpart", [P, 2, 3, TT // 2], BF16)
        crow = sb("crow", [3 * TT // 2, 2, P], BF16)
        recip = sb("recip", [P, NQ, 4])
        ewt = sb("ewt", [P, NFT, TOPK])
        eix = sb("eix", [P, NFT, TOPK], I32)
        eixf = sb("eixf", [P, NFT, TOPK])
        wtok = sb("wtok", [P, E, NFT])

        bv_bc, bo_bc = wqkv[:, 0, 3 * D:4 * D], wqkv[:, 0, 4 * D:5 * D]
        xT = xT_f[:, :].rearrange("p (k n) -> p k n", k=KD)
        oh = xT_f[:, :].rearrange("p (t d) -> p t d", d=D)
        parts = parts_f[:, :].bitcast(BF16).rearrange("p (a n) -> p a n", n=L)
        stacks = stack_f[:, :].bitcast(BF16).rearrange("p (a n) -> p a n", n=L)
        qf, res, rot1, rot2 = (probs[:, 2 * i:2 * i + 2, :] for i in range(4))
        epick = probs[:, 0, 0:E * NFT * TOPK].rearrange("p (e t k) -> p e t k", e=E, t=NFT)
        o_t = acc_sb[:, :, 0:D]
        staged = parts_f[:, 12 * L // 2 - TT * D:].rearrange("p (t d) -> p t d", d=D)
        w1_sb = stack_f[:, 0:2 * KD * FF].rearrange("p (s k f) -> p s k f", s=2, k=KD)
        w2_sb = stack_f[:, 2 * KD * FF:].rearrange("p (s f d) -> p s f d", s=2, f=NF)
        hid = parts_f[:, 0:2 * NF * QW].rearrange("p (s f n) -> p s f n", s=2, f=NF)
        facc = v_all[:, 0:NFT, :]

        def part(proj, half, i):
            return parts[:, (half * 2 + proj) * 3 + i, :]

        def q_stack(s):
            return stacks[:, 2 * s, :]

        def k_stack(s):
            return stacks[:, 2 * s + 1, :]

        ps_s = ctx.enter_context(nc.psum_tensor("ps_s", [P, 3, QW], F32))
        ps_m = ctx.enter_context(nc.psum_tensor("ps_m", [P, MBANKS, QW], F32))
        ps_acc = ctx.enter_context(nc.psum_tensor("ps_acc", [P, QW], F32))
        ps_o = ctx.enter_context(nc.psum_tensor("ps_o", [P, QW], F32))
        c_ps = [ps_m[:, i, 0:P // 2].bitcast(BF16) for i in range(MBANKS)]

        def ring(i):
            return (ps_s[:, 0, :], ps_s[:, 1, :], ps_s[:, 2, :], ps_acc[:, :])[i % 4]

        def y_bank(t):
            return (ps_m[:, 0, 0:D], ps_m[:, 1, 0:D], ps_m[:, 2, 0:D], ps_o[:, 0:D])[t]

        def s_bank(j, n):
            return (n + j) % 3, (1, 4, 4)[n] if j == 0 and n < 3 else 3

        passed = sem("passed")
        consts_in = sem("consts_in")
        weights_in = sem("weights_in")
        xb_in = sem("xb_in")
        xn_in = sem("xn_in")
        x_stored = sem("x_stored")
        ones_in = sem("ones_in")
        q_scaled = sem("q_scaled")
        stack_in = [sem(f"stack_in{s}") for s in range(SLOTS)]
        rows_in = [[sem(f"rows_in{g}{s}") for s in range(SLOTS)] for g in range(2)]
        dve_step = sem("dve_step")
        pool_step = sem("pool_step")
        var_ready = sem("var_ready")
        sd_ready = sem("sd_ready")
        rstd_out = sem("rstd_out")
        xn_ready = sem("xn_ready")
        xn_turned = sem("xn_turned")
        xT_ready = sem("xT_ready")
        v_mm = sem("v_mm")
        v_ready = sem("v_ready")
        qk_mm = sem("qk_mm")
        rotated = sem("rotated")
        roped = sem("roped")
        part1_out = sem("part1_out")
        res_out = sem("res_out")
        part2_out = sem("part2_out")
        qk_split = sem("qk_split")
        item_mm = sem("item_mm")
        item_used = sem("item_used")
        m_ready = sem("m_ready")
        c_ready = sem("c_ready")
        v_head_ready = sem("v_head_ready")
        s_mm = sem("s_mm")
        exp_done = sem("exp_done")
        pv_mm = sem("pv_mm")
        acc_out = sem("acc_out")
        sum_mm = sem("sum_mm")
        sum_out = sem("sum_out")
        o_mm = sem("o_mm")
        recip_out = sem("recip_out")
        o_norm = sem("o_norm")
        stack_free = sem("stack_free")
        ot_mm = sem("ot_mm")
        ot_out = sem("ot_out")
        y_mm = sem("y_mm")
        y_added = sem("y_added")
        x_ready = sem("x_ready")
        x_staged = sem("x_staged")
        ffn_out = sem("ffn_out")
        facc_zero = sem("facc_zero")
        ew_in = [sem("ew_in0"), sem("ew_in1")]
        h_mm = sem("h_mm")
        gelu_out = sem("gelu_out")
        fy_mm = sem("fy_mm")
        fy_added = sem("fy_added")

        prod_row = (POS, 0)
        c_row = (POS + 16 * NPART, 16 * NPART)

        assert H == TT == 4 * NQ

        def upto(per, ly, b16, n, more=0):
            return b16 * per + (per * (ly * B * H + n) + more)

        def item_count(ly, hb, h, at):
            if h is None:
                return upto(ITEMS, ly, hb, 0, at)
            return upto(ITEMS, ly, hb, h, len(FIRST_STREAM) + at)

        def turned(ly, b16, n):
            return b16 + (ly * (B * TT + NFT) + n)

        def item_at(more, n):
            return sum(len(x) for x in stream(more)[:n])

        def freed(ly, b16, kind, i):
            return ((res_out, rotated)[ly] if kind == "q" else v_ready,
                    b16 + (i + 1 if ly and kind == "q" else ly * B * TT + i + 1))

        block = ctx.enter_context(nc.Block())

        @block.sync
        def _(sp):
            for dst, src in ((identf[:, :], ident_in[0]), (identb[:, :], ident_in[1]), (mask[:, :], mask_in[0]), (early[:, :], mask_in[1]),
                             (sel[:, :], sel_in), (bv_bc, bv_a), (bo_bc, bo_a), (fb_bc[:, :], fbias),
                             (bqk[:, :, :], bqk_a), (cosb[:, :], cos_t), (sinb[:, :], sin_t),
                             (ewt[:, :, :], e_w.rearrange("(t p) k -> p t k", p=P)),
                             (eix[:, :, :], e_idx.rearrange("(t p) k -> p t k", p=P))):
                sp.dma_start(dst, src).then_inc(consts_in, 16)

            def weights(ly):
                w, w_o = ((w_a, wo_a), (w_b, wo_b))[ly]
                n = w.shape[1]
                sp.dma_start(wqkv[:, :, 0:n], w.rearrange("(k p) n -> p k n", p=P)).then_inc(weights_in, 16)
                sp.dma_start(wo[:, :, :], w_o.rearrange("(k p) n -> p k n", p=P)).then_inc(weights_in, 16)
                for s in range(SLOTS):
                    sp.dma_start(k_stack(s)[c_row[ly]:c_row[ly] + 3, :], ones_rows).then_inc(ones_in, 16)

            def load_stack(ly, b16, h):
                s = h % SLOTS
                half, r = h // 8, 16 * (h % 8)
                sp.wait_ge(stack_free, upto(1, ly, b16, h, 1))
                sp.sem_inc(passed, 1)
                if h % 8 == 0:
                    sp.wait_ge(qk_split, upto(1, ly, b16, 8 * half + 8))
                for stack, source, proj in ((q_stack(s), Q_PARTS, 0), (k_stack(s), K_PARTS, 1)):
                    for g, i in enumerate(source):
                        to = prod_row[ly] + 16 * g
                        sp.dma_start(stack[to:to + 16, :], part(proj, half, i)[r:r + 16, :]).then_inc(stack_in[s], 16)
                if ly == 0:
                    sp.dma_start(q_stack(s)[0:POS, :], q_pos[h]).then_inc(stack_in[s], 16)
                    sp.dma_start(k_stack(s)[0:POS, :], k_pos[h]).then_inc(stack_in[s], 16)

            def load_rows(ly, b16, h, g):
                s = h % SLOTS
                first = (TT // 2 * P, 0)[g]
                if g:
                    before = item_count(ly, b16, h, LO_STEP + 1 if h + 1 < H else 0)
                elif h == 0:
                    before = item_count(ly, b16, None, FIRST_HI)
                else:
                    before = item_count(ly, b16, h - 1, HI_STEP + 2)
                sp.wait_ge(item_used, before + 1)
                for i in range(3):
                    row = q_stack(s)[c_row[ly] + i:c_row[ly] + i + 1, first:first + TT // 2 * P]
                    sp.dma_start(row, crow[TT // 2 * i:TT // 2 * (i + 1), g, :]).then_inc(rows_in[g][s], 16)

            def rows_of(x, b, n=TT):
                return x.rearrange("(b t p) d -> p b t d", p=P, t=n)[:, bass.ds(b, 1), :, :]\
                    .rearrange("p o t d -> p (o t) d")

            def expert_weights(e, s):
                sp.dma_start(w1_sb[:, s, :, :], w1[bass.ds(e, 1), :, :]
                             .rearrange("o (k p) f -> p (o k) f", p=P)).then_inc(ew_in[s], 16)
                sp.dma_start(w2_sb[:, s, :, :], w2[bass.ds(e, 1), :, :]
                             .rearrange("o (f p) d -> p (o f) d", p=P)).then_inc(ew_in[s], 16)

            stored = 32 * B + 16

            def batch(ly, b, last):
                b16 = b * TT
                x_from = (x_in, x_a)[ly]
                for h in range(3):
                    load_stack(ly, b16, h)
                load_rows(ly, b16, 0, 0)
                load_rows(ly, b16, 0, 1)
                sp.wait_ge(x_stored, b * 32 + (ly * stored + 1))
                sp.sem_inc(passed, 1)
                sp.dma_start(xb[:, :, :], rows_of(x_from, b)).then_inc(xb_in, 16)
                sp.wait_ge(xn_turned, turned(ly, b16, TT))
                sp.sem_inc(passed, 1)
                if last:
                    sp.dma_start(xn[:, 0:NFT, :], rows_of(x_raw, ROUTED, NFT)).then_inc(xn_in, 16)
                else:
                    sp.dma_start(xn[:, :, :], rows_of(x_from, b + 1)).then_inc(xn_in, 16)
                for h in range(H):
                    if h + 3 < H:
                        load_stack(ly, b16, h + 3)
                    if h + 1 < H:
                        load_rows(ly, b16, h + 1, 0)
                        load_rows(ly, b16, h + 1, 1)
                if last:
                    sp.wait_ge(stack_free, upto(1, ly, b16, H, SLOTS))
                    expert_weights(0, 0)
                    expert_weights(1, 1)
                sp.wait_ge((x_ready, y_added)[ly], upto(1, ly, b16, TT))
                sp.sem_inc(passed, 1)
                sp.dma_start(rows_of(x_raw, b, NFT), xb[:, 0:NFT, :]).then_inc(x_stored, 16)
                sp.wait_ge(x_staged, upto(1, ly, b16, TT))
                sp.sem_inc(passed, 1)
                sp.dma_start(rows_of((x_a, out)[ly], b), staged).then_inc(x_stored, 16)

            for ly in range(2):
                weights(ly)
                if ly == 0:
                    sp.dma_start(xn[:, :, :], rows_of(x_in, 0)).then_inc(xn_in, 16)
                with sp.Fori(0, B - 1) as b:
                    batch(ly, b, False)
                batch(ly, B - 1, True)
                sp.wait_ge(x_stored, ly * stored + 32 * B + 1)
                sp.dma_start(xb[:, 0:NFT, :], rows_of(x_raw, ROUTED, NFT)).then_inc(xb_in, 16)
                if ly == 0:
                    sp.wait_ge(xn_turned, B * TT + NFT)
                    sp.dma_start(xn[:, :, :], rows_of(x_a, 0)).then_inc(xn_in, 16)
                with sp.Fori(1, E // 2) as ep:
                    for s in range(2):
                        sp.wait_ge(fy_mm, ly * E * NFT + ep * 2 * NFT + (s - 1) * NFT)
                        sp.sem_inc(passed, 1)
                        expert_weights(2 * ep + s, s)
                sp.wait_ge(ffn_out, (ly + 1) * NFT)
                to = (x_a, out)[ly][ROUTED * L:ROUTED * L + FT, :].rearrange("(t p) d -> p t d", p=P)
                sp.dma_start(to, xb[:, 0:NFT, :]).then_inc(x_stored, 16)
                sp.wait_ge(x_stored, (ly + 1) * stored + 1)

        @block.gpsimd
        def _(pool):
            pool.memset(v_head[:, :, :, :], 1.0).then_inc(pool_step, 1)
            pool.memset(zeros[:, :], 0.0).then_inc(pool_step, 1)
            pool.wait_ge(pool_step, 2)
            steps = 2
            per_group = 3

            def copy_v_head(slot, h):
                pool.sem_inc(passed, 1)
                pool.tensor_copy(v_head[:, slot, :, 0:DH], v_all[:, :, bass.ds(DH * h, DH)])\
                    .then_inc(v_head_ready, 1)

            def split_max(ly, hb, h, g):
                cols = (slice(TT // 2, TT), slice(0, TT // 2))[g]
                pool.wait_ge(m_ready, upto(2, ly, hb, h, g + 1))
                pool.sem_inc(passed, 1)
                pool.tensor_copy(cpart[:, g, 0, :], negmax[:, cols]).then_inc(pool_step, 1)
                pool.wait_ge(pool_step, upto(2 * per_group, ly, hb, h, steps + g * per_group + 1))
                pool.tensor_tensor(cres[:, g, :], negmax[:, cols], cpart[:, g, 0, :], ALU.subtract)\
                    .then_inc(pool_step, 1)
                pool.wait_ge(pool_step, upto(2 * per_group, ly, hb, h, steps + g * per_group + 2))
                pool.sem_inc(passed, 1)
                pool.tensor_copy(cpart[:, g, 1, :], cres[:, g, :]).then_inc(pool_step, 1)
                pool.wait_ge(pool_step, upto(2 * per_group, ly, hb, h, steps + g * per_group + 3))
                pool.tensor_tensor(cpart[:, g, 2, :], cres[:, g, :], cpart[:, g, 1, :], ALU.subtract)\
                    .then_inc(c_ready, 1)

            def head(ly, hb, h, slot, col_head):
                split_max(ly, hb, h, 0)
                split_max(ly, hb, h, 1)
                copy_v_head(slot, col_head)

            for ly in range(2):
                with pool.Fori(0, B) as b:
                    b16 = b * TT
                    for u in range(4 * NQ):
                        if ly:
                            pool.wait_ge(rotated, b16 + (u + 1))
                            if u >= 2:
                                pool.wait_ge(res_out, upto(1, ly, b16, u - 1))
                            pool.tensor_tensor(qf[:, u % 2, :], rot1[:, u % 2, :], rot2[:, u % 2, :], ALU.add)\
                                .then_inc(roped, 1)
                        else:
                            half, proj, n = u // 8, u // 4 % 2, u % 4
                            p2, p3 = (part(proj, half, i)[:, n * QW:(n + 1) * QW] for i in (1, 2))
                            pool.wait_ge(part2_out, upto(1, ly, b16, u + 1))
                            pool.tensor_tensor(p3, res[:, u % 2, :], p2, ALU.subtract).then_inc(qk_split, 1)
                        if u == 13:
                            split_max(ly, b16, 0, 0)
                    pool.wait_ge(v_ready, upto(1, ly, b16, TT))
                    copy_v_head(0, 0)
                    split_max(ly, b16, 0, 1)
                    with pool.Fori(0, (H - 2) // 2) as i:
                        hb = b16 + 2 * i
                        for j in range(2):
                            head(ly, hb, j + 1, (j + 1) % 2, 2 * i + j + 1)
                    head(ly, b16, H - 1, (H - 1) % 2, H - 1)
                    for t in range(TT):
                        pool.wait_ge((x_ready, y_added)[ly], upto(1, ly, b16, t + 1))
                        pool.tensor_tensor(staged[:, t, :], xb[:, t, :], fb_bc[:, :], ALU.add).then_inc(x_staged, 1)
                pool.wait_ge(xb_in, 16 * (ly + 1) * (B + 1))
                done = steps + (ly + 1) * 2 * B * H * per_group
                for t in range(NFT):
                    pool.wait_ge(fy_added, (ly + 1) * E * NFT + 1)
                    pool.tensor_tensor(xb[:, t, :], xb[:, t, :], facc[:, t, :], ALU.add).then_inc(pool_step, 1)
                for t in range(NFT):
                    pool.wait_ge(pool_step, done + t + 1)
                    pool.tensor_tensor(xb[:, t, :], xb[:, t, :], fb_bc[:, :], ALU.add).then_inc(ffn_out, 1)
                steps += NFT

        @block.scalar
        def _(act):
            def turn_out(ly, b16, n):
                for t in range(n):
                    act.wait_ge(xn_turned, turned(ly, b16, t + 1))
                    act.activation(xT[:, :, t * P:(t + 1) * P],
                                   ps_m[:, t % MBANKS, 0:D].rearrange("p (k n) -> p k n", k=KD), ACT.Copy)\
                        .then_inc(xT_ready, 1)

            def std(norm):
                act.wait_ge(var_ready, norm + 1)
                act.activation(sd[:, :], vpe[:, :], ACT.Sqrt).then_inc(sd_ready, 1)

            def acc_evac(ly, hb, h, qt):
                act.wait_ge(pv_mm, upto(GROUPS, ly, hb, h, {3: 4, 2: 7, 1: 9, 0: 10}[qt]))
                if qt == NQ - 1:
                    act.wait_ge(sum_mm, upto(1, ly, hb, h, 1))
                act.activation(acc_sb[:, qt, :], ps_acc[:, :], ACT.Copy).then_inc(acc_out, 1)

            def exp_block(ly, hb, h, j, n, opening):
                qt, kb, q0 = BLOCK[n]
                act.wait_ge(s_mm, upto(BLOCKS, ly, hb, h, n + 1))
                if not opening:
                    act.wait_ge(pv_mm, upto(GROUPS, ly, hb, h, n // 4 - 1))
                act.activation(probs[:, n % 8, 0:QW - q0], ps_s[:, s_bank(j, n)[0], q0:QW], ACT.Exp)\
                    .then_inc(exp_done, 1)

            def head(ly, hb, h, j, more, after):
                for dh, n in steps_of(h):
                    if not dh or more:
                        exp_block(ly, hb, h + dh, (j + dh) % GROUP, n, False)
                    if not dh and n in ACC_STEP:
                        acc_evac(ly, hb, h, ACC_STEP[n])
                    if not more and not dh and n == 28:
                        std(after)
                    if dh and n == 3:
                        acc_evac(ly, hb, h, 0)
                    if dh and n == SUM_STEP + 1:
                        act.wait_ge(sum_mm, upto(1, ly, hb, h, 2))
                        act.activation(osum[:, :], ps_o[:, :], ACT.Copy).then_inc(sum_out, 1)

            def place(u, i):
                half, proj, n = u // 8, u // 4 % 2, u % 4
                return part(proj, half, i)[:, n * QW:(n + 1) * QW]

            def part1(ly, b16, u):
                half, proj = u // 8, u // 4 % 2
                if u == 2 * NQ:
                    act.wait_ge(x_stored, b16 * 2 + (ly * (32 * B + 16) + 1))
                if ly == 0:
                    act.wait_ge(qk_mm, upto(1, ly, b16, u + 1))
                    act.activation(place(u, 0), ring(JOBS.index(("q", u))), ACT.Identity,
                                   bias=bqk[:, proj, half:half + 1]).then_inc(part1_out, 1)
                else:
                    act.wait_ge(roped, b16 + (u + 1))
                    act.activation(place(u, 0), qf[:, u % 2, :], ACT.Copy).then_inc(part1_out, 1)

            def part2(ly, b16, u):
                act.wait_ge(res_out, upto(1, ly, b16, u + 1))
                act.activation(place(u, 1), res[:, u % 2, :], ACT.Copy).then_inc(part2_out, 1)

            act.wait_ge(consts_in, CONSTS)
            act.activation(bqk[:, 0, :], bqk[:, 0, :], ACT.Copy, scale=DH ** -0.5).then_inc(q_scaled, 1)
            for ly in range(2):
                act.wait_ge(weights_in, 32 * (ly + 1))
                for at in ((0,), (0, 3 * D))[ly]:
                    act.activation(wqkv[:, :, at:at + D], wqkv[:, :, at:at + D], ACT.Copy, scale=DH ** -0.5)\
                        .then_inc(q_scaled, 1)
                if ly == 0:
                    act.wait_ge(q_scaled, 1)
                if ly == 0:
                    std(0)
                with act.Fori(0, B) as b:
                    b16 = b * TT
                    turn_out(ly, b16, TT)
                    for kind, i in PROJECTIONS:
                        if kind == "v" and ly:
                            act.wait_ge(v_mm, upto(1, ly, b16, i + 1))
                            act.activation(v_all[:, i, :], ring(2 * JOBS.index((kind, i)))[:, 0:D], ACT.Copy)\
                                .then_inc(v_ready, 1)
                        if kind == "q":
                            if i % (2 * NQ) >= ly:
                                part1(ly, b16, i - ly)
                            if i % (2 * NQ) >= ly + 1:
                                part2(ly, b16, i - ly - 1)
                            if i % (2 * NQ) == 2 * NQ - 1:
                                for k in range(i - ly + 1, i + 1):
                                    part2(ly, b16, k - 1)
                                    part1(ly, b16, k)
                                part2(ly, b16, i)
                    act.wait_ge(qk_split, upto(1, ly, b16, TT))
                    for n in range(ROT):
                        exp_block(ly, b16, 0, 0, n, True)
                    with act.Fori(0, H // GROUP - 1) as i:
                        hb = b16 + GROUP * i
                        for j in range(GROUP):
                            head(ly, hb, j, j, True, None)
                    for j in range(GROUP):
                        h = H - GROUP + j
                        head(ly, b16, h, j, h + 1 < H, b + (ly * (B + 1) + 1))
                    for t in range(TT):
                        act.wait_ge(ot_mm, upto(1, ly, b16, t + 1))
                        if t >= 4:
                            act.wait_ge(y_mm, upto(1, ly, b16, t - 3))
                        act.activation(o_t[:, t % 4, :], ps_m[:, t % MBANKS, 0:D], ACT.Copy).then_inc(ot_out, 1)
                turn_out(ly, B * TT, NFT)
                if ly == 0:
                    std(B + 1)
                with act.Fori(0, E // 2) as ep:
                    for s in range(2):
                        for n in range(2):
                            step = ep * 4 + (ly * E * 2 + 2 * s + n)
                            for f in range(NF):
                                act.wait_ge(h_mm, step * NF + f + 1)
                                act.activation(hid[:, n, f, :], ring(f), ACT.Gelu).then_inc(gelu_out, 1)

        @block.tensor
        def _(pe):
            pe.wait_ge(consts_in, CONSTS)
            pe.wait_ge(pool_step, 2)
            pe.sem_inc(stack_free, SLOTS)
            for done in (acc_out, sum_mm, o_norm, x_stored, fy_added):
                pe.sem_inc(done, 1)

            def turn_xn(ly, b16, n):
                for t in range(n):
                    pe.wait_ge(xn_ready, b16 + (ly * (B + 1) * TT + t + 1))
                    if t >= MBANKS:
                        pe.wait_ge(xT_ready, turned(ly, b16, t - MBANKS + 1))
                    for k in range(KD):
                        mm = pe.transpose(ps_m[:, t % MBANKS, k * P:(k + 1) * P], xn[:, t, k * P:(k + 1) * P],
                                          identf[:, :])
                    mm.then_inc(xn_turned, 1)

            def project(ly, b16, job):
                kind, i = JOBS[job]
                back = (4, 2)[ly]
                if job >= back:
                    pe.wait_ge(*freed(ly, b16, *JOBS[job - back]))
                if kind == "v":
                    to = ring(job * (1, 2)[ly])
                    for k in range(KD):
                        mm = pe.matmul(to[:, 0:D], xT[:, k, i * P:(i + 1) * P], wqkv[:, k, 2 * D:3 * D],
                                       start=(k == 0), stop=(k == KD - 1))
                    mm.then_inc(v_mm, 1)
                    return
                half, proj, n = i // 8, i // 4 % 2, i % 4
                if half == proj == 0:
                    pe.wait_ge(xT_ready, turned(ly, b16, 4 * n + 4))
                outs = ((job, proj * D),) if ly == 0 else ((2 * job, proj * D), (2 * job + 1, (3 + proj) * D))
                for bank, at in outs:
                    at += half * P
                    for k in range(KD):
                        mm = pe.matmul(ring(bank), wqkv[:, k, at:at + P], xT[:, k, n * QW:(n + 1) * QW],
                                       start=(k == 0), stop=(k == KD - 1))
                mm.then_inc(qk_mm, 1)

            def item(ly, hb, h, at, what, slot):
                before = item_count(ly, hb, h, at)
                bank = (len(FIRST_STREAM) * (h is not None) + at) % MBANKS
                nxt = 0 if h is None else h + 1
                if what in (LO, HI):
                    g, of = (1, h) if what == LO else (0, nxt)
                    pe.wait_ge(c_ready, upto(2, ly, hb, of, g + 1))
                if h is not None or at >= MBANKS:
                    pe.wait_ge(item_used, before - MBANKS + 1)
                if what in (LO, HI):
                    pe.transpose(c_ps[bank][0:3 * TT // 2, :], cpart[:, g, :, :].rearrange("p i t -> p (i t)"),
                                 identb[:, :]).then_inc(item_mm, 1)
                    return
                qb, kc, w = UNIT[what]
                rows = c_row[ly]
                if what == 0:
                    pe.wait_ge(stack_in[slot], stack_count(ly, hb, nxt, slot))
                pe.matmul(ps_m[:, bank, 0:w], q_stack(slot)[0:rows, qb * P:(qb + 1) * P],
                          k_stack(slot)[0:rows, kc * QW:kc * QW + w], start=True, stop=True).then_inc(item_mm, 1)

            def stack_count(ly, hb, h, slot):
                per_a, per_b = 16 * (LOADS + 2), 16 * LOADS
                per = (per_a, per_b)[ly]
                before = per_a * B * (H // SLOTS) if ly else 0
                return hb * (per // SLOTS) + (before + per // SLOTS * (h - slot) + per)

            def rows_count(ly, hb, h, slot):
                per = 16 * 3
                return hb * (per // SLOTS) + per // SLOTS * (ly * B * H + h - slot + SLOTS)

            def scores(ly, hb, h, n, slot, opening):
                qt, kb, q0 = BLOCK[n]
                rows = c_row[ly] + 3
                bank, back = s_bank(slot, n)
                if n == 0:
                    pe.wait_ge(rows_in[0][slot], rows_count(ly, hb, h, slot))
                if n == FIRST_LO:
                    pe.wait_ge(rows_in[1][slot], rows_count(ly, hb, h, slot))
                if not opening or n >= 3:
                    pe.wait_ge(exp_done, upto(BLOCKS, ly, hb, h, n - back + 1))
                mm = pe.matmul(ps_s[:, bank, q0:QW], k_stack(slot)[0:rows, kb * P:(kb + 1) * P],
                               q_stack(slot)[0:rows, qt * QW + q0:(qt + 1) * QW], start=True, stop=True)
                if kb >= 4 * qt:
                    mm = pe.matmul(ps_s[:, bank, q0:q0 + P], identb[:, :], early[:, :], start=False, stop=True,
                                   skip_group_check=True)
                mm.then_inc(s_mm, 1)

            def times_v(ly, hb, h, g, slot):
                fresh = g in FIRST_GROUP
                if fresh:
                    pe.wait_ge(acc_out, upto(NQ, ly, hb, h, NQ - FIRST_GROUP[g]))
                if g == GROUPS - 1:
                    pe.matmul(ps_acc[:, :], zeros[0:P // 2, :], q_stack(slot)[0:P // 2, 0:QW], start=True, stop=False,
                              skip_group_check=True).then_inc(stack_free, 1)
                    fresh = False
                pe.wait_ge(exp_done, upto(BLOCKS, ly, hb, h, 4 * g + 4))
                if g == 0:
                    pe.wait_ge(v_head_ready, upto(1, ly, hb, h, 1))
                pieces = [(r, r, BLOCK[4 * g + r][2], QW) for r in range(4)]
                if g in LAST_GROUP:
                    pieces[0] = (0, 0, 0, QW - P)
                    pieces.append((0, 3, QW - P, QW))
                for r, tile, lo, hi in pieces:
                    n = 4 * g + r
                    _, kb, q0 = BLOCK[n]
                    mm = pe.matmul(ps_acc[32 * tile:32 * tile + 32, lo:hi], v_head[:, slot % 2, kb, :],
                                   probs[:, n % 8, lo - q0:hi - q0], start=fresh, stop=g in LAST_GROUP,
                                   skip_group_check=True)
                mm.then_inc(pv_mm, 1)

            def sum_up(ly, hb, h):
                pe.wait_ge(acc_out, upto(NQ, ly, hb, h, NQ + 1))
                pe.wait_ge(o_norm, upto(1, ly, hb, h, 1))
                for qt in range(NQ):
                    mm = pe.matmul(ps_o[32 * qt:32 * qt + 32, :], sel[:, :], acc_sb[:, qt, :], start=True, stop=True)
                mm.then_inc(sum_mm, 1)

            def turn_sum(ly, hb, h):
                pe.wait_ge(sum_out, upto(1, ly, hb, h, 1))
                for c in range(4):
                    mm = pe.transpose(ps_o[:, c * P:(c + 1) * P], osum[:, c * P:(c + 1) * P], identf[:, :])
                mm.then_inc(o_mm, 1)

            def one_block(ly, hb, h, n, slot, more, opening):
                scores(ly, hb, h, n, slot, opening)
                at = item_at(more, n)
                for what in stream(more)[n]:
                    item(ly, hb, h, at, what, (slot + 1) % SLOTS)
                    at += 1
                if n >= PV_LAG and (n - PV_LAG) % 4 == 0:
                    times_v(ly, hb, h, (n - PV_LAG) // 4, slot)

            def head(ly, hb, h, slot, more, more2):
                for dh, n in steps_of(h):
                    if not dh:
                        one_block(ly, hb, h, n, slot, more, False)
                        continue
                    if more:
                        one_block(ly, hb, h + 1, n, (slot + 1) % SLOTS, more2, False)
                    if 4 * (GROUPS - 1) + PV_LAG - BLOCKS == n:
                        times_v(ly, hb, h, GROUPS - 1, slot)
                    if n == SUM_STEP:
                        sum_up(ly, hb, h)
                    if n == TURN_STEP:
                        turn_sum(ly, hb, h)

            for ly in range(2):
                pe.wait_ge(weights_in, 32 * (ly + 1))
                pe.wait_ge(q_scaled, (2, 4)[ly])
                pe.wait_ge(ones_in, 16 * SLOTS * (ly + 1))
                with pe.Fori(0, B) as b:
                    b16 = b * TT
                    turn_xn(ly, b16, TT)
                    job = 0
                    for kind, i in PROJECTIONS:
                        if kind == "m":
                            item(ly, b16, None, i, FIRST_STREAM[i], 0)
                        else:
                            project(ly, b16, job)
                            job += 1
                    pe.wait_ge(v_ready, upto(1, ly, b16, TT))
                    pe.wait_ge(*freed(ly, b16, "q", 4 * NQ - 1))
                    for n in range(ROT):
                        one_block(ly, b16, 0, n, 0, True, True)
                    with pe.Fori(0, H // GROUP - 1) as i:
                        hb = b16 + GROUP * i
                        for j in range(GROUP):
                            head(ly, hb, j, j, True, True)
                    for j in range(GROUP):
                        h = H - GROUP + j
                        head(ly, b16, h, j, h + 1 < H, h + 2 < H)
                    pe.wait_ge(o_norm, upto(1, ly, b16, H, 1))
                    for t in range(TT + 2):
                        if t < TT:
                            if t >= MBANKS:
                                pe.wait_ge(ot_out, upto(1, ly, b16, t - MBANKS + 1))
                            for k in range(KD):
                                mm = pe.transpose(ps_m[:, t % MBANKS, k * P:(k + 1) * P], oh[:, t, k * P:(k + 1) * P],
                                                  identf[:, :])
                            mm.then_inc(ot_mm, 1)
                        if t >= 2:
                            pe.wait_ge(ot_out, upto(1, ly, b16, t - 1))
                            if t - 2 >= 4:
                                pe.wait_ge(y_added, upto(1, ly, b16, t - 5))
                            for k in range(KD):
                                mm = pe.matmul(ring(t - 2)[:, 0:D], o_t[:, (t - 2) % 4, k * P:(k + 1) * P],
                                               wo[:, k, :], start=(k == 0), stop=(k == KD - 1))
                            mm.then_inc(y_mm, 1)
                    pe.wait_ge(y_added, upto(1, ly, b16, TT))
                turn_xn(ly, B * TT, NFT)
                pe.wait_ge(xT_ready, turned(ly, B * TT, NFT))
                with pe.Fori(0, E // 2) as ep:
                    for s in range(2):
                        pe.wait_ge(ew_in[s], 32 * (ly * (E // 2) + ep + 1))
                        for n in range(2):
                            step = ep * 4 + (ly * E * 2 + 2 * s + n)
                            for f in range(NF):
                                if f >= 4:
                                    pe.wait_ge(gelu_out, step * NF + f - 3)
                                for k in range(KD):
                                    mm = pe.matmul(ring(f), w1_sb[:, s, k, f * P:(f + 1) * P],
                                                   xT[:, k, n * QW:(n + 1) * QW], start=(k == 0), stop=(k == KD - 1))
                                mm.then_inc(h_mm, 1)
                            pe.wait_ge(fy_added, step * 4 + 1)
                            for t in range(4):
                                for f in range(NF):
                                    if t == 0:
                                        pe.wait_ge(gelu_out, step * NF + f + 1)
                                    mm = pe.matmul(y_bank(t), hid[:, n, f, t * P:(t + 1) * P],
                                                   w2_sb[:, s, f, :], start=(f == 0), stop=(f == NF - 1))
                                mm.then_inc(fy_mm, 1)
                pe.wait_ge(fy_added, (ly + 1) * E * NFT + 1)

        @block.vector
        def _(dve):
            dve.memset(part_max[:, :, :], LOWEST).then_inc(dve_step, 1)
            dve.wait_ge(consts_in, CONSTS)
            dve.tensor_copy(eixf[:, :, :], eix[:, :, :]).then_inc(dve_step, 1)
            dve.wait_ge(dve_step, 2)
            for e in range(E):
                dve.scalar_tensor_tensor(out=epick[:, e, :, :], in0=eixf[:, :, :], scalar=float(e), in1=ewt[:, :, :],
                                         op0=ALU.is_equal, op1=ALU.mult).then_inc(dve_step, 1)
            dve.wait_ge(dve_step, 2 + E)
            dve.tensor_tensor(wtok[:, :, :], epick[:, :, :, 0], epick[:, :, :, 1], ALU.add).then_inc(dve_step, 1)
            dve.wait_ge(dve_step, 3 + E)
            setup_steps = 3 + E
            ln_steps = 6

            def norm(nth):
                def base(k):
                    return nth * ln_steps + (setup_steps + k)

                dve.wait_ge(xn_in, nth * 16 + 16)
                for t in range(TT):
                    mm = dve.bn_stats(stats[:, t, :], xn[:, t, :])
                mm.then_inc(dve_step, 1)
                dve.wait_ge(dve_step, base(1))
                dve.sem_inc(passed, 1)
                for t in range(TT):
                    mm = dve.bn_aggr(mv[:, t, :], stats[:, t, :])
                mm.then_inc(dve_step, 1)
                dve.wait_ge(dve_step, base(2))
                dve.tensor_scalar_add(vpe[:, :], mv[:, :, 1], EPS).then_inc(var_ready, 1)
                dve.wait_ge(sd_ready, nth + 1)
                dve.reciprocal(r0[:, :], sd[:, :]).then_inc(dve_step, 1)
                dve.wait_ge(dve_step, base(3))
                dve.tensor_tensor(r1[:, :], r0[:, :], r0[:, :], ALU.mult).then_inc(dve_step, 1)
                dve.wait_ge(dve_step, base(4))
                dve.tensor_tensor(r1[:, :], r1[:, :], vpe[:, :], ALU.mult).then_inc(dve_step, 1)
                dve.wait_ge(dve_step, base(5))
                dve.tensor_scalar(r1[:, :], r1[:, :], -0.5, 1.5, ALU.mult, ALU.add).then_inc(dve_step, 1)
                dve.wait_ge(dve_step, base(6))
                dve.tensor_tensor(rstd[:, :], r0[:, :], r1[:, :], ALU.mult).then_inc(rstd_out, 1)
                dve.wait_ge(rstd_out, nth + 1)
                for t in range(TT):
                    dve.tensor_scalar(xn[:, t, :], xn[:, t, :], mv[:, t, 0:1], rstd[:, t:t + 1],
                                      ALU.subtract, ALU.mult).then_inc(xn_ready, 1)

            def use_item(ly, hb, h, at, what):
                before = item_count(ly, hb, h, at)
                bank = (len(FIRST_STREAM) * (h is not None) + at) % MBANKS
                dve.wait_ge(item_mm, before + 1)
                if what in (LO, HI):
                    g = (1, 0)[what == HI]
                    dve.tensor_copy(crow[:, g, :], c_ps[bank][0:3 * TT // 2, :]).then_inc(item_used, 1)
                    return
                qb, kc, w = UNIT[what]
                if kc == qb // 4:
                    dve.sem_inc(passed, 1)
                    dve.tensor_tensor_reduce(ps_m[:, bank, 0:w], ps_m[:, bank, 0:w], mask[:, QW - w:QW], 1.0, LOWEST,
                                             ALU.add, ALU.max, part_max[:, qb, kc:kc + 1]).then_inc(item_used, 1)
                else:
                    dve.reduce_max(part_max[:, qb, kc:kc + 1], ps_m[:, bank, 0:w], AX_X).then_inc(item_used, 1)
                if what + 1 in (HI_UNITS, UNITS):
                    g = (HI_UNITS, UNITS).index(what + 1)
                    cols = (slice(TT // 2, TT), slice(0, TT // 2))[g]
                    dve.wait_ge(item_used, before + 1)
                    dve.tensor_reduce(negmax[:, cols], part_max[:, cols, :], AX_X, ALU.max, negate=True)\
                        .then_inc(m_ready, 1)

            def beside(ly, hb, h, more, n):
                at = item_at(more, n)
                for what in stream(more)[n]:
                    use_item(ly, hb, h, at, what)
                    at += 1

            def normalise(ly, hb, h, col):
                o = ps_o[:, :].rearrange("p (c q d) -> p q c d", c=4, q=NQ)
                dve.wait_ge(o_mm, upto(1, ly, hb, h, 1))
                dve.reciprocal(recip[:, :, :], o[:, :, :, DH]).then_inc(recip_out, 1)
                dve.wait_ge(recip_out, upto(1, ly, hb, h, 1))
                dve.tensor_tensor(oh[:, :, bass.ds(col, DH)].rearrange("p (q c) d -> p q c d", c=4), o[:, :, :, 0:DH],
                                  recip[:, :, :].rearrange("p q (c o) -> p q c o", o=1).broadcast_to([P, NQ, 4, DH]),
                                  ALU.mult).then_inc(o_norm, 1)

            def head(ly, hb, h, more, more2, col, nth):
                if not more:
                    for n in range(ROT, BLOCKS):
                        beside(ly, hb, h, more, n)
                    norm(nth)
                for dh, n in steps_of(h):
                    if dh and more:
                        beside(ly, hb, h + 1, more2, n)
                    if not dh and more:
                        beside(ly, hb, h, more, n)
                normalise(ly, hb, h, col)

            def rotate(b16, u):
                n = u % 4
                cols = slice(n * QW, (n + 1) * QW)
                job = JOBS.index(("q", u))
                dve.wait_ge(qk_mm, upto(1, 1, b16, u + 1))
                if u >= 2:
                    dve.wait_ge(roped, b16 + (u - 1))
                dve.tensor_tensor(rot1[:, u % 2, :], ring(2 * job), cosb[:, cols], ALU.mult)
                dve.tensor_tensor(rot2[:, u % 2, :], ring(2 * job + 1), sinb[:, cols], ALU.mult).then_inc(rotated, 1)

            def place(u, i):
                half, proj, n = u // 8, u // 4 % 2, u % 4
                return part(proj, half, i)[:, n * QW:(n + 1) * QW]

            def rest(ly, b16, u):
                half, proj = u // 8, u // 4 % 2
                dve.wait_ge(part1_out, upto(1, ly, b16, u + 1))
                if u >= 2:
                    dve.wait_ge(qk_split, upto(1, ly, b16, u - 1))
                if ly == 0:
                    dve.scalar_tensor_tensor(out=res[:, u % 2, :], in0=ring(JOBS.index(("q", u))),
                                             scalar=bqk[:, proj, half:half + 1], in1=place(u, 0),
                                             op0=ALU.add, op1=ALU.subtract).then_inc(res_out, 1)
                else:
                    dve.tensor_tensor(res[:, u % 2, :], qf[:, u % 2, :], place(u, 0), ALU.subtract)\
                        .then_inc(res_out, 1)

            def part3(b16, u):
                dve.wait_ge(part2_out, upto(1, 1, b16, u + 1))
                dve.tensor_tensor(place(u, 2), res[:, u % 2, :], place(u, 1), ALU.subtract).then_inc(qk_split, 1)

            norm(0)
            for ly in range(2):
                with dve.Fori(0, B) as b:
                    b16 = b * TT
                    for kind, i in PROJECTIONS:
                        if kind == "m":
                            use_item(ly, b16, None, i, FIRST_STREAM[i])
                        elif kind == "v" and ly == 0:
                            dve.wait_ge(v_mm, upto(1, ly, b16, i + 1))
                            dve.tensor_tensor(v_all[:, i, :], ring(JOBS.index((kind, i)))[:, 0:D], bv_bc, ALU.add)\
                                .then_inc(v_ready, 1)
                        elif kind == "q" and ly == 0:
                            rest(ly, b16, i)
                        elif kind == "q":
                            rotate(b16, i)
                            if i % 8 >= 1:
                                rest(ly, b16, i - 1)
                            if i % 8 >= 2:
                                part3(b16, i - 2)
                            if i % 8 == 7:
                                part3(b16, i - 1)
                                rest(ly, b16, i)
                                part3(b16, i)
                    for n in range(ROT):
                        beside(ly, b16, 0, True, n)
                    with dve.Fori(0, H // GROUP - 1) as i:
                        hb = b16 + GROUP * i
                        for j in range(GROUP):
                            head(ly, hb, j, True, True, DH * GROUP * i + DH * j, None)
                    for h in range(H - GROUP, H):
                        head(ly, b16, h, h + 1 < H, h + 2 < H, DH * h, b + (ly * (B + 1) + 1))
                    dve.wait_ge(xb_in, 16 * (b + 1) + 16 * ly * (B + 1))
                    for t in range(TT + 1):
                        if t < TT:
                            dve.wait_ge(y_mm, upto(1, ly, b16, t + 1))
                            dve.tensor_tensor(xb[:, t, :], xb[:, t, :], ring(t)[:, 0:D], ALU.add)\
                                .then_inc(y_added, 1)
                        if ly == 0 and t >= 1:
                            dve.wait_ge(y_added, upto(1, ly, b16, t))
                            dve.tensor_tensor(xb[:, t - 1, :], xb[:, t - 1, :], bo_bc, ALU.add)\
                                .then_inc(x_ready, 1)

                dve.memset(facc, 0.0).then_inc(facc_zero, 1)
                dve.wait_ge(facc_zero, ly + 1)
                if ly == 0:
                    norm(B + 1)
                with dve.Fori(0, E // 2) as ep:
                    for s in range(2):
                        for n in range(2):
                            step = ep * 4 + (ly * E * 2 + 2 * s + n)
                            for t in range(4):
                                tile = 4 * n + t
                                dve.wait_ge(fy_mm, step * 4 + t + 1)
                                dve.scalar_tensor_tensor(out=facc[:, tile, :], in0=y_bank(t),
                                                         scalar=wtok[:, bass.ds(2 * ep + s, 1), tile],
                                                         in1=facc[:, tile, :], op0=ALU.mult, op1=ALU.add)\
                                    .then_inc(fy_added, 1)


def kernel(**inputs):
    import ml_dtypes
    import concourse.bacc as bacc
    from concourse.bass_utils import run_bass_kernel_spmd as run

    bf = ml_dtypes.bfloat16
    g = {k: np.asarray(v) for k, v in inputs.items()}
    x = np.roll(g["L0_attn_a_x"], ROUTED, axis=0).reshape(B * L, D)
    w_a = np.concatenate([g["L0_attn_a_Wq"].T, g["L0_attn_a_Wk"].T, g["L0_attn_a_Wv"].T], axis=1)
    kqv = g["L0_attn_b_W_KQV"]
    wk, wq, wv = kqv[0:D], kqv[D:2 * D], kqv[2 * D:]
    swap = np.arange(D) ^ 1
    w_b = np.concatenate([wq.T, wk.T, wv.T, wq[swap].T, wk[swap].T], axis=1)
    bqk = np.stack([g["L0_attn_a_bq"].reshape(KD, P).T, g["L0_attn_a_bk"].reshape(KD, P).T], axis=1)

    pos = np.arange(L)
    inv = (1.0 / np.float32(10000.0) ** (np.arange(0, DH, 2, dtype=np.float32) / np.float32(DH))).astype(np.float32)
    freqs = (pos.astype(np.float32)[:, None] * inv[None, :]).astype(np.float32)
    feat = np.arange(P) % DH
    cos_t = np.cos(freqs).astype(np.float32)[:, feat // 2].T
    sin_t = (np.sin(freqs).astype(np.float32)[:, feat // 2] * np.where(feat % 2, 1, -1)).T.astype(np.float32)
    slopes = np.power(np.float32(2.0), (np.float32(-8.0) * np.arange(1, H + 1, dtype=np.float32) / np.float32(H)))
    slopes = slopes.astype(np.float32)
    cut, rest = [], slopes.copy()
    for _ in range(3):
        s = rest.astype(bf)
        cut.append(s.astype(np.float32))
        rest = (rest - cut[-1]).astype(np.float32)
    q_pos = np.zeros((H, POS, L), np.float32)
    k_pos = np.zeros((H, POS, L), np.float32)
    for i in range(3):
        for u, p in enumerate((pos // P * P, pos % P)):
            q_pos[:, 4 * i + 2 * u] = p
            k_pos[:, 4 * i + 2 * u] = -cut[i][:, None]
            q_pos[:, 4 * i + 2 * u + 1] = cut[i][:, None]
            k_pos[:, 4 * i + 2 * u + 1] = p
    eye = np.eye(P, dtype=np.float32)
    r, c = np.arange(P)[:, None], np.arange(P)[None, :]
    mask = np.zeros((P, QW), np.float32)
    mask[:, QW - P:] = np.where(c > r, MASKED, 0.0)
    early = np.where(r > c, MASKED, 0.0)
    sel = np.zeros((P, 2 * DH), np.float32)
    for q in range(4):
        for d in range(DH + 1):
            sel[2 * DH * q + d, d] = 1.0

    def rows(v):
        return np.ascontiguousarray(np.broadcast_to(v[None, :], (P, D)))

    arrays = {
        "x_in": x, "w_a": w_a, "wo_a": g["L0_attn_a_Wo"].T, "bqk_a": bqk, "bv_a": rows(g["L0_attn_a_bv"]),
        "bo_a": rows(g["L0_attn_a_bo"]), "w_b": w_b, "wo_b": g["L0_attn_b_W_O"].T, "cos_t": cos_t, "sin_t": sin_t,
        "q_pos": q_pos.astype(bf), "k_pos": k_pos.astype(bf), "ones_rows": np.ones((3, L), bf),
        "ident_f": eye, "ident_b": eye.astype(bf), "late_keys": mask.astype(bf), "early_queries": early.astype(bf), "sel_in": sel,
        "e_w": g["L0_ffn_expert_weights"], "e_idx": g["L0_ffn_expert_indices"],
        "w1": g["L0_ffn_w1"], "w2": g["L0_ffn_w2"], "fbias": rows(g["L0_ffn_bias"]),
    }
    nc = bacc.Bacc("TRN2", target_bir_lowering=False, num_devices=1)
    aps, maps = {}, {}
    for name, a in arrays.items():
        a = np.ascontiguousarray(a)
        maps[name + "_dram"] = a
        aps[name] = nc.dram_tensor(name + "_dram", a.shape, mybir.dt.from_np(a.dtype), kind="ExternalInput").ap()
    aps["ident_in"] = (aps.pop("ident_f"), aps.pop("ident_b"))
    aps["mask_in"] = (aps.pop("late_keys"), aps.pop("early_queries"))
    aps["out"] = nc.dram_tensor("out_dram", (B * L, D), F32, kind="ExternalOutput").ap()
    build(nc, **aps)
    res = run(nc, [maps], core_ids=[0])
    return np.roll(res.results[0]["out_dram"].reshape(B, L, D), -ROUTED, axis=0)
```

```python
from contextlib import ExitStack

import numpy as np

import concourse.bass as bass
from concourse import mybir

F32 = mybir.dt.float32
BF16 = mybir.dt.bfloat16
I32 = mybir.dt.int32
ALU = mybir.AluOpType
ACT = mybir.ActivationFunctionType
AX_X = mybir.AxisListType.X

P = 128
B, L, D = 4, 2048, 256
H, DH = 16, 16
KD = D // P
TT = L // P
QW = 512
NQ = L // QW
E, FF, TOPK = 8, 1024, 2
FT = 1024
NFT = FT // P
NF = FF // P
ET = 2 * P
ETILES = (FT * TOPK + E * (ET - 1)) // ET
assert ETILES % 2
J = NFT * TOPK
ROUTED = 2
EPS = 1e-5
MASKED = -1e30
LOWEST = -3.0e38

SLOTS = 4
GROUP = 4
NPART = 6
Q_PARTS = (0, 0, 0, 1, 1, 2)
K_PARTS = (0, 1, 2, 0, 1, 0)
POS = 12

UNITS = sum(4 * (qt + 1) for qt in range(NQ))
BLOCKS = sum(4 * (qt + 1) for qt in range(NQ))
LOADS = 2 * NPART
CONSTS = 16 * 15

BLOCK = [(qt, kb, max(0, P * (kb - 4 * qt))) for qt in reversed(range(NQ)) for kb in range(4 * qt + 4)]
UNIT = [(qb, kc, QW if kc < qt else P * (qb - 4 * qt + 1))
        for qt in reversed(range(NQ)) for qb in range(4 * qt, 4 * qt + 4) for kc in range(qt + 1)]
HI_UNITS = sum(1 for qb, _, _ in UNIT if qb >= TT // 2)
LO, HI = -1, -2
LO_STEP, HI_STEP = 5, 32
FIRST_LO = next(n for n, x in enumerate(BLOCK) if x[0] == 1)


def stream(with_next):
    return [([n] if with_next else []) + ([LO] if n == LO_STEP else []) +
            ([HI] if with_next and n == HI_STEP else []) for n in range(BLOCKS)]


FIRST_HI = 36
FIRST_STREAM = list(range(FIRST_HI)) + [HI] + list(range(FIRST_HI, UNITS))
ITEMS = UNITS + 2
MBANKS = 3
assert ITEMS % MBANKS == 0
LAST_GROUP = {3: 3, 6: 2, 8: 1, 9: 0}
FIRST_GROUP = {0: 3, 4: 2, 7: 1, 9: 0}
GROUPS = BLOCKS // 4

ROT = 8
PV_LAG = 6
SUM_STEP, TURN_STEP = 5, 7
ACC_STEP = {19: 3, 31: 2, 39: 1}


def steps_of(h):
    return [(0, n) for n in range(ROT, BLOCKS)] + [(1, n) for n in range(ROT)]


def projections():
    seq = [("q", u) for u in range(2 * NQ)] + [("v", t) for t in range(TT // 2)]
    rest = [x for i in range(TT // 2) for x in (("v", TT // 2 + i), ("q", 2 * NQ + i))]
    done = 0
    for i, x in enumerate(rest):
        seq.append(x)
        while done < len(FIRST_STREAM) * (i + 1) // len(rest):
            seq.append(("m", done))
            done += 1
    return seq


PROJECTIONS = projections()
JOBS = [x for x in PROJECTIONS if x[0] != "m"]


def build(nc, x_in, w_a, wo_a, bqk_a, bv_a, bo_a, w_b, wo_b, tri_in, ramp_in, cos_t, sin_t, q_pos, k_pos, ones_rows,
          ident_in, mask_in, sel_in, e_w, e_idx, w1, w2, fbias, out):
    x_a = nc.dram_tensor("x_after_a", (B * L, D), F32, kind="Internal").ap()
    x_raw = nc.dram_tensor("x_before_ffn", (B * FT, D), F32, kind="Internal").ap()
    xs = nc.dram_tensor("rows_by_expert", (ETILES * ET, D), F32, kind="Internal").ap()
    ys = nc.dram_tensor("ffn_by_expert", (ETILES * ET, D), F32, kind="Internal").ap()

    with ExitStack() as ctx:
        def sb(name, shape, dt=F32):
            return ctx.enter_context(nc.sbuf_tensor(name, shape, dt))

        def sem(name):
            return ctx.enter_context(nc.semaphore(name))

        xb = sb("xb", [P, TT, D])
        xn = sb("xn", [P, TT, D])
        xT_f = sb("xT", [P, KD * L])
        parts_f = sb("parts", [P, 12 * L // 2])
        stack_f = sb("stacks", [P, 2 * SLOTS * L // 2])
        v_all = sb("v_all", [P, TT, D])
        v_head = sb("v_head", [P, 2, TT, 2 * DH])
        probs = sb("probs", [P, 8, QW])
        acc_sb = sb("acc_sb", [P, NQ, QW])
        osum = sb("osum", [P, QW])
        wqkv = sb("wqkv", [P, KD, 5 * D])
        wo = sb("wo", [P, KD, D])
        cosb = sb("cosb", [P, L])
        sinb = sb("sinb", [P, L])
        fb_bc = sb("fb_bc", [P, D])
        bqk = sb("bqk", [P, 2, KD])
        identf = sb("identf", [P, P])
        identb = sb("identb", [P, P], BF16)
        mask = sb("mask", [P, QW], BF16)
        early = sb("early", [P, P], BF16)
        sel = sb("sel", [P, 2 * DH])
        zeros = sb("zeros", [P, P], BF16)
        stats = sb("stats", [P, TT, 6])
        mv = sb("mv", [P, TT, 2])
        vpe = sb("vpe", [P, TT])
        sd = sb("sd", [P, TT])
        r0 = sb("r0", [P, TT])
        r1 = sb("r1", [P, TT])
        rstd = sb("rstd", [P, TT])
        part_max = sb("part_max", [P, TT, NQ])
        negmax = sb("negmax", [P, TT])
        cres = sb("cres", [P, 2, TT // 2])
        cpart = sb("cpart", [P, 2, 3, TT // 2], BF16)
        crow = sb("crow", [3 * TT // 2, 2, P], BF16)
        recip = sb("recip", [P, NQ, 4])
        ewt = sb("ewt", [P, NFT, TOPK])
        eix = sb("eix", [P, NFT, TOPK], I32)
        slot_of = sb("slot_of", [P, J], I32)
        expert_of = sb("expert_of", [P, ETILES], I32)

        bv_bc, bo_bc = wqkv[:, 0, 3 * D:4 * D], wqkv[:, 0, 4 * D:5 * D]
        xT = xT_f[:, :].rearrange("p (k n) -> p k n", k=KD)
        oh = xT_f[:, :].rearrange("p (t d) -> p t d", d=D)
        parts = parts_f[:, :].bitcast(BF16).rearrange("p (a n) -> p a n", n=L)
        stacks = stack_f[:, :].bitcast(BF16).rearrange("p (a n) -> p a n", n=L)
        qf, res, rot1, rot2 = (probs[:, 2 * i:2 * i + 2, :] for i in range(4))
        tri, all_ones = probs[:, 1, 0:P], probs[:, 1, P:2 * P]
        choice = probs[:, 0, 0:J]
        onehot, before, rank = (probs[:, 2 + i, 0:E * J].rearrange("p (e j) -> p e j", e=E) for i in range(3))
        n_of, tiles_of, tiles_to, base_of = (probs[:, 5, i * E:(i + 1) * E] for i in range(4))
        slot_f, expert_f, ramp = (probs[:, 6, i * J:i * J + n] for i, n in enumerate((J, ETILES, ETILES)))
        o_t = acc_sb[:, :, 0:D]
        staged = parts_f[:, 12 * L // 2 - TT * D:].rearrange("p (t d) -> p t d", d=D)
        w1_sb = stack_f[:, 0:2 * KD * FF].rearrange("p (s k f) -> p s k f", s=2, k=KD)
        w2_sb = stack_f[:, 2 * KD * FF:].rearrange("p (s f d) -> p s f d", s=2, f=NF)
        hid = parts_f[:, 0:NF * ET].rearrange("p (f n) -> p f n", f=NF)
        xs_sb, xsT, ys_sb = (parts_f[:, NF * ET + i * 4 * D:NF * ET + (i + 1) * 4 * D]
                             .rearrange("p (s c n) -> p s c n", s=2, c=2) for i in range(3))
        picked = v_all

        def part(proj, half, i):
            return parts[:, (half * 2 + proj) * 3 + i, :]

        def q_stack(s):
            return stacks[:, 2 * s, :]

        def k_stack(s):
            return stacks[:, 2 * s + 1, :]

        ps_s = ctx.enter_context(nc.psum_tensor("ps_s", [P, 3, QW], F32))
        ps_m = ctx.enter_context(nc.psum_tensor("ps_m", [P, MBANKS, QW], F32))
        ps_acc = ctx.enter_context(nc.psum_tensor("ps_acc", [P, QW], F32))
        ps_o = ctx.enter_context(nc.psum_tensor("ps_o", [P, QW], F32))
        c_ps = [ps_m[:, i, 0:P // 2].bitcast(BF16) for i in range(MBANKS)]

        def ring(i):
            return (ps_s[:, 0, :], ps_s[:, 1, :], ps_s[:, 2, :], ps_acc[:, :])[i % 4]

        y_bank = (ps_m[:, 2, 0:D], ps_o[:, 0:D])

        def s_bank(j, n):
            return (n + j) % 3, (1, 4, 4)[n] if j == 0 and n < 3 else 3

        passed = sem("passed")
        consts_in = sem("consts_in")
        weights_in = sem("weights_in")
        xb_in = sem("xb_in")
        xn_in = sem("xn_in")
        x_stored = sem("x_stored")
        ones_in = sem("ones_in")
        q_scaled = sem("q_scaled")
        stack_in = [sem(f"stack_in{s}") for s in range(SLOTS)]
        rows_in = [[sem(f"rows_in{g}{s}") for s in range(SLOTS)] for g in range(2)]
        dve_step = sem("dve_step")
        pool_step = sem("pool_step")
        var_ready = sem("var_ready")
        sd_ready = sem("sd_ready")
        rstd_out = sem("rstd_out")
        xn_ready = sem("xn_ready")
        xn_turned = sem("xn_turned")
        xT_ready = sem("xT_ready")
        v_mm = sem("v_mm")
        v_ready = sem("v_ready")
        qk_mm = sem("qk_mm")
        rotated = sem("rotated")
        roped = sem("roped")
        part1_out = sem("part1_out")
        res_out = sem("res_out")
        part2_out = sem("part2_out")
        qk_split = sem("qk_split")
        item_mm = sem("item_mm")
        item_used = sem("item_used")
        m_ready = sem("m_ready")
        c_ready = sem("c_ready")
        v_head_ready = sem("v_head_ready")
        s_mm = sem("s_mm")
        exp_done = sem("exp_done")
        pv_mm = sem("pv_mm")
        acc_out = sem("acc_out")
        sum_mm = sem("sum_mm")
        sum_out = sem("sum_out")
        o_mm = sem("o_mm")
        recip_out = sem("recip_out")
        o_norm = sem("o_norm")
        stack_free = sem("stack_free")
        ot_mm = sem("ot_mm")
        ot_out = sem("ot_out")
        y_mm = sem("y_mm")
        y_added = sem("y_added")
        x_ready = sem("x_ready")
        x_staged = sem("x_staged")
        ffn_out = sem("ffn_out")
        onehot_ready = sem("onehot_ready")
        ranks_mm = sem("ranks_mm")
        table_ready = sem("table_ready")
        xs_zeroed = sem("xs_zeroed")
        xs_scattered = sem("xs_scattered")
        xs_in = [sem("xs_in0"), sem("xs_in1")]
        xs_turned = sem("xs_turned")
        xsT_ready = sem("xsT_ready")
        ys_out = sem("ys_out")
        ys_stored = [sem("ys_stored0"), sem("ys_stored1")]
        picked_in = [sem("picked_in0"), sem("picked_in1")]
        mixed = sem("mixed")
        ew_in = [sem("ew_in0"), sem("ew_in1")]
        h_mm = sem("h_mm")
        gelu_out = sem("gelu_out")
        fy_mm = sem("fy_mm")

        prod_row = (POS, 0)
        c_row = (POS + 16 * NPART, 16 * NPART)

        assert H == TT == 4 * NQ

        def upto(per, ly, b16, n, more=0):
            return b16 * per + (per * (ly * B * H + n) + more)

        def item_count(ly, hb, h, at):
            if h is None:
                return upto(ITEMS, ly, hb, 0, at)
            return upto(ITEMS, ly, hb, h, len(FIRST_STREAM) + at)

        def turned(ly, b16, n):
            return b16 + (ly * B * TT + n)

        def item_at(more, n):
            return sum(len(x) for x in stream(more)[:n])

        def freed(ly, b16, kind, i):
            return ((res_out, rotated)[ly] if kind == "q" else v_ready,
                    b16 + (i + 1 if ly and kind == "q" else ly * B * TT + i + 1))

        block = ctx.enter_context(nc.Block())

        @block.sync
        def _(sp):
            for dst, src in ((identf[:, :], ident_in[0]), (identb[:, :], ident_in[1]), (mask[:, :], mask_in[0]), (early[:, :], mask_in[1]),
                             (sel[:, :], sel_in), (bv_bc, bv_a), (bo_bc, bo_a), (fb_bc[:, :], fbias),
                             (bqk[:, :, :], bqk_a), (tri, tri_in), (ramp, ramp_in), (cosb[:, :], cos_t), (sinb[:, :], sin_t),
                             (ewt[:, :, :], e_w.rearrange("(t p) k -> p t k", p=P)),
                             (eix[:, :, :], e_idx.rearrange("(t p) k -> p t k", p=P))):
                sp.dma_start(dst, src).then_inc(consts_in, 16)

            def weights(ly):
                w, w_o = ((w_a, wo_a), (w_b, wo_b))[ly]
                n = w.shape[1]
                sp.dma_start(wqkv[:, :, 0:n], w.rearrange("(k p) n -> p k n", p=P)).then_inc(weights_in, 16)
                sp.dma_start(wo[:, :, :], w_o.rearrange("(k p) n -> p k n", p=P)).then_inc(weights_in, 16)
                for s in range(SLOTS):
                    sp.dma_start(k_stack(s)[c_row[ly]:c_row[ly] + 3, :], ones_rows).then_inc(ones_in, 16)

            def load_stack(ly, b16, h):
                s = h % SLOTS
                half, r = h // 8, 16 * (h % 8)
                sp.wait_ge(stack_free, upto(1, ly, b16, h, 1))
                sp.sem_inc(passed, 1)
                if h % 8 == 0:
                    sp.wait_ge(qk_split, upto(1, ly, b16, 8 * half + 8))
                for stack, source, proj in ((q_stack(s), Q_PARTS, 0), (k_stack(s), K_PARTS, 1)):
                    for g, i in enumerate(source):
                        to = prod_row[ly] + 16 * g
                        sp.dma_start(stack[to:to + 16, :], part(proj, half, i)[r:r + 16, :]).then_inc(stack_in[s], 16)
                if ly == 0:
                    sp.dma_start(q_stack(s)[0:POS, :], q_pos[h]).then_inc(stack_in[s], 16)
                    sp.dma_start(k_stack(s)[0:POS, :], k_pos[h]).then_inc(stack_in[s], 16)

            def load_rows(ly, b16, h, g):
                s = h % SLOTS
                first = (TT // 2 * P, 0)[g]
                if g:
                    before = item_count(ly, b16, h, LO_STEP + 1 if h + 1 < H else 0)
                elif h == 0:
                    before = item_count(ly, b16, None, FIRST_HI)
                else:
                    before = item_count(ly, b16, h - 1, HI_STEP + 2)
                sp.wait_ge(item_used, before + 1)
                for i in range(3):
                    row = q_stack(s)[c_row[ly] + i:c_row[ly] + i + 1, first:first + TT // 2 * P]
                    sp.dma_start(row, crow[TT // 2 * i:TT // 2 * (i + 1), g, :]).then_inc(rows_in[g][s], 16)

            def rows_of(x, b, n=TT):
                return x.rearrange("(b t p) d -> p b t d", p=P, t=n)[:, bass.ds(b, 1), :, :]\
                    .rearrange("p o t d -> p (o t) d")

            sp.wait_ge(pool_step, 3)
            for i in range(2):
                rows = slice(i * (ETILES * ET // 2), (i + 1) * (ETILES * ET // 2))
                sp.dma_start(xs[rows, :].rearrange("(p t) d -> p (t d)", p=P), xT_f[:, 0:ETILES * ET // 2 // P * D])\
                    .then_inc(xs_zeroed, 16)

            def expert_weights(i, s):
                e = sp.value_load(expert_of[0:1, bass.ds(i, 1)], min_val=0, max_val=E - 1)
                sp.dma_start(w1_sb[:, s, :, :], w1[bass.ds(e, 1), :, :]
                             .rearrange("o (k p) f -> p (o k) f", p=P)).then_inc(ew_in[s], 16)
                sp.dma_start(w2_sb[:, s, :, :], w2[bass.ds(e, 1), :, :]
                             .rearrange("o (f p) d -> p (o f) d", p=P)).then_inc(ew_in[s], 16)

            def slots(x, i):
                return x.rearrange("(i c p) d -> p i c d", p=P, c=2)[:, bass.ds(i, 1), :, :]\
                    .rearrange("p o c d -> p (o c) d")

            def store_ys(ly, i, s):
                sp.wait_ge(ys_out, 2 * i + (ly * 2 * ETILES + 3))
                sp.sem_inc(passed, 1)
                sp.dma_start(slots(ys, i), ys_sb[:, s, :, :]).then_inc(ys_stored[s], 16)

            stored = 32 * B + 16

            def batch(ly, b, last):
                b16 = b * TT
                x_from = (x_in, x_a)[ly]
                for h in range(3):
                    load_stack(ly, b16, h)
                load_rows(ly, b16, 0, 0)
                load_rows(ly, b16, 0, 1)
                sp.wait_ge(x_stored, b * 32 + (ly * stored + 1))
                sp.sem_inc(passed, 1)
                sp.dma_start(xb[:, :, :], rows_of(x_from, b)).then_inc(xb_in, 16)
                sp.wait_ge(xn_turned, turned(ly, b16, TT))
                sp.sem_inc(passed, 1)
                if last:
                    sp.dma_start(xn[:, 0:NFT, :], rows_of(x_raw, ROUTED, NFT)).then_inc(xn_in, 16)
                else:
                    sp.dma_start(xn[:, :, :], rows_of(x_from, b + 1)).then_inc(xn_in, 16)
                for h in range(H):
                    if h + 3 < H:
                        load_stack(ly, b16, h + 3)
                    if h + 1 < H:
                        load_rows(ly, b16, h + 1, 0)
                        load_rows(ly, b16, h + 1, 1)
                if last:
                    sp.wait_ge(stack_free, upto(1, ly, b16, H, SLOTS))
                    sp.wait_ge(table_ready, 2)
                    expert_weights(0, 0)
                    expert_weights(1, 1)
                sp.wait_ge((x_ready, y_added)[ly], upto(1, ly, b16, TT))
                sp.sem_inc(passed, 1)
                sp.dma_start(rows_of(x_raw, b, NFT), xb[:, 0:NFT, :]).then_inc(x_stored, 16)
                sp.wait_ge(x_staged, upto(1, ly, b16, TT))
                sp.sem_inc(passed, 1)
                sp.dma_start(rows_of((x_a, out)[ly], b), staged).then_inc(x_stored, 16)

            for ly in range(2):
                weights(ly)
                if ly == 0:
                    sp.dma_start(xn[:, :, :], rows_of(x_in, 0)).then_inc(xn_in, 16)
                with sp.Fori(0, B - 1) as b:
                    batch(ly, b, False)
                batch(ly, B - 1, True)
                for s in range(2):
                    if s == 0:
                        sp.wait_ge(xs_scattered, (ly + 1) * 16 * J)
                    sp.dma_start(xs_sb[:, s, :, :], slots(xs, s)).then_inc(xs_in[s], 16)
                sp.wait_ge(x_stored, ly * stored + 32 * B + 1)
                sp.dma_start(xb[:, 0:NFT, :], rows_of(x_raw, ROUTED, NFT)).then_inc(xb_in, 16)
                if ly == 0:
                    sp.dma_start(xn[:, :, :], rows_of(x_a, 0)).then_inc(xn_in, 16)

                def next_tile(i, s):
                    sp.wait_ge(fy_mm, 2 * i + (ly * 2 * ETILES - 2))
                    sp.sem_inc(passed, 1)
                    sp.dma_start(xs_sb[:, s, :, :], slots(xs, i)).then_inc(xs_in[s], 16)
                    expert_weights(i, s)
                    store_ys(ly, i - 2, s)

                with sp.Fori(1, ETILES // 2) as ip:
                    for s in range(2):
                        next_tile(2 * ip + s, s)
                next_tile(ETILES - 1, 0)
                store_ys(ly, ETILES - 2, 1)
                store_ys(ly, ETILES - 1, 0)
                sp.wait_ge(ffn_out, (ly + 1) * NFT)
                to = (x_a, out)[ly][ROUTED * L:ROUTED * L + FT, :].rearrange("(t p) d -> p t d", p=P)
                sp.dma_start(to, xb[:, 0:NFT, :]).then_inc(x_stored, 16)
                sp.wait_ge(x_stored, (ly + 1) * stored + 1)

        @block.gpsimd
        def _(pool):
            pool.memset(v_head[:, :, :, :], 1.0).then_inc(pool_step, 1)
            pool.memset(zeros[:, :], 0.0).then_inc(pool_step, 1)
            pool.memset(xT_f[:, :], 0.0).then_inc(pool_step, 1)
            pool.wait_ge(pool_step, 3)
            steps = 3
            per_group = 3

            def copy_v_head(slot, h):
                pool.sem_inc(passed, 1)
                pool.tensor_copy(v_head[:, slot, :, 0:DH], v_all[:, :, bass.ds(DH * h, DH)])\
                    .then_inc(v_head_ready, 1)

            def split_max(ly, hb, h, g):
                cols = (slice(TT // 2, TT), slice(0, TT // 2))[g]
                pool.wait_ge(m_ready, upto(2, ly, hb, h, g + 1))
                pool.sem_inc(passed, 1)
                pool.tensor_copy(cpart[:, g, 0, :], negmax[:, cols]).then_inc(pool_step, 1)
                pool.wait_ge(pool_step, upto(2 * per_group, ly, hb, h, steps + g * per_group + 1))
                pool.tensor_tensor(cres[:, g, :], negmax[:, cols], cpart[:, g, 0, :], ALU.subtract)\
                    .then_inc(pool_step, 1)
                pool.wait_ge(pool_step, upto(2 * per_group, ly, hb, h, steps + g * per_group + 2))
                pool.sem_inc(passed, 1)
                pool.tensor_copy(cpart[:, g, 1, :], cres[:, g, :]).then_inc(pool_step, 1)
                pool.wait_ge(pool_step, upto(2 * per_group, ly, hb, h, steps + g * per_group + 3))
                pool.tensor_tensor(cpart[:, g, 2, :], cres[:, g, :], cpart[:, g, 1, :], ALU.subtract)\
                    .then_inc(c_ready, 1)

            def head(ly, hb, h, slot, col_head):
                split_max(ly, hb, h, 0)
                split_max(ly, hb, h, 1)
                copy_v_head(slot, col_head)

            def batch(ly, b, last):
                b16 = b * TT
                for u in range(4 * NQ):
                    if ly:
                        pool.wait_ge(rotated, b16 + (u + 1))
                        if u >= 2:
                            pool.wait_ge(res_out, upto(1, ly, b16, u - 1))
                        pool.tensor_tensor(qf[:, u % 2, :], rot1[:, u % 2, :], rot2[:, u % 2, :], ALU.add)\
                            .then_inc(roped, 1)
                    else:
                        half, proj, n = u // 8, u // 4 % 2, u % 4
                        p2, p3 = (part(proj, half, i)[:, n * QW:(n + 1) * QW] for i in (1, 2))
                        pool.wait_ge(part2_out, upto(1, ly, b16, u + 1))
                        pool.tensor_tensor(p3, res[:, u % 2, :], p2, ALU.subtract).then_inc(qk_split, 1)
                    if u == 13:
                        split_max(ly, b16, 0, 0)
                pool.wait_ge(v_ready, upto(1, ly, b16, TT))
                copy_v_head(0, 0)
                split_max(ly, b16, 0, 1)
                with pool.Fori(0, (H - 2) // 2) as i:
                    hb = b16 + 2 * i
                    for j in range(2):
                        head(ly, hb, j + 1, (j + 1) % 2, 2 * i + j + 1)
                head(ly, b16, H - 1, (H - 1) % 2, H - 1)
                if last:
                    pool.wait_ge(table_ready, 2)
                    pool.wait_ge(xs_zeroed, 32)
                    pool.wait_ge(xn_ready, (ly + 1) * (B + 1) * TT)
                    for j in range(J):
                        pool.indirect_dma_start(xs[:, :], bass.IndirectOffsetOnAxis(ap=slot_of[:, j:j + 1], axis=0),
                                                xn[:, j // TOPK, :], None).then_inc(xs_scattered, 16)
                for t in range(TT):
                    pool.wait_ge((x_ready, y_added)[ly], upto(1, ly, b16, t + 1))
                    pool.tensor_tensor(staged[:, t, :], xb[:, t, :], fb_bc[:, :], ALU.add).then_inc(x_staged, 1)

            for ly in range(2):
                with pool.Fori(0, B - 1) as b:
                    batch(ly, b, False)
                batch(ly, B - 1, True)
                for s in range(2):
                    pool.wait_ge(ys_stored[s], 16 + 16 * ((ETILES + 1 - s) // 2) * (ly + 1))
                for j in range(J):
                    j = j % NFT * TOPK + j // NFT
                    pool.indirect_dma_start(picked[:, j, :], None, ys[:, :],
                                            bass.IndirectOffsetOnAxis(ap=slot_of[:, j:j + 1], axis=0))\
                        .then_inc(picked_in[j % TOPK], 16)

        @block.scalar
        def _(act):
            def turn_out(ly, b16, n):
                for t in range(n):
                    act.wait_ge(xn_turned, turned(ly, b16, t + 1))
                    act.activation(xT[:, :, t * P:(t + 1) * P],
                                   ps_m[:, t % MBANKS, 0:D].rearrange("p (k n) -> p k n", k=KD), ACT.Copy)\
                        .then_inc(xT_ready, 1)

            def std(norm):
                act.wait_ge(var_ready, norm + 1)
                act.activation(sd[:, :], vpe[:, :], ACT.Sqrt).then_inc(sd_ready, 1)

            def acc_evac(ly, hb, h, qt):
                act.wait_ge(pv_mm, upto(GROUPS, ly, hb, h, {3: 4, 2: 7, 1: 9, 0: 10}[qt]))
                if qt == NQ - 1:
                    act.wait_ge(sum_mm, upto(1, ly, hb, h, 1))
                act.activation(acc_sb[:, qt, :], ps_acc[:, :], ACT.Copy).then_inc(acc_out, 1)

            def exp_block(ly, hb, h, j, n, opening):
                qt, kb, q0 = BLOCK[n]
                act.wait_ge(s_mm, upto(BLOCKS, ly, hb, h, n + 1))
                if not opening:
                    act.wait_ge(pv_mm, upto(GROUPS, ly, hb, h, n // 4 - 1))
                act.activation(probs[:, n % 8, 0:QW - q0], ps_s[:, s_bank(j, n)[0], q0:QW], ACT.Exp)\
                    .then_inc(exp_done, 1)

            def head(ly, hb, h, j, more, after):
                for dh, n in steps_of(h):
                    if not dh or more:
                        exp_block(ly, hb, h + dh, (j + dh) % GROUP, n, False)
                    if not dh and n in ACC_STEP:
                        acc_evac(ly, hb, h, ACC_STEP[n])
                    if not more and not dh and n == 28:
                        std(after)
                    if dh and n == 3:
                        acc_evac(ly, hb, h, 0)
                    if dh and n == SUM_STEP + 1:
                        act.wait_ge(sum_mm, upto(1, ly, hb, h, 2))
                        act.activation(osum[:, :], ps_o[:, :], ACT.Copy).then_inc(sum_out, 1)

            def place(u, i):
                half, proj, n = u // 8, u // 4 % 2, u % 4
                return part(proj, half, i)[:, n * QW:(n + 1) * QW]

            def part1(ly, b16, u):
                half, proj = u // 8, u // 4 % 2
                if u == 2 * NQ:
                    act.wait_ge(x_stored, b16 * 2 + (ly * (32 * B + 16) + 1))
                if ly == 0:
                    act.wait_ge(qk_mm, upto(1, ly, b16, u + 1))
                    act.activation(place(u, 0), ring(JOBS.index(("q", u))), ACT.Identity,
                                   bias=bqk[:, proj, half:half + 1]).then_inc(part1_out, 1)
                else:
                    act.wait_ge(roped, b16 + (u + 1))
                    act.activation(place(u, 0), qf[:, u % 2, :], ACT.Copy).then_inc(part1_out, 1)

            def part2(ly, b16, u):
                act.wait_ge(res_out, upto(1, ly, b16, u + 1))
                act.activation(place(u, 1), res[:, u % 2, :], ACT.Copy).then_inc(part2_out, 1)

            act.wait_ge(consts_in, CONSTS)
            act.activation(bqk[:, 0, :], bqk[:, 0, :], ACT.Copy, scale=DH ** -0.5).then_inc(q_scaled, 1)
            for ly in range(2):
                act.wait_ge(weights_in, 32 * (ly + 1))
                for at in ((0,), (0, 3 * D))[ly]:
                    act.activation(wqkv[:, :, at:at + D], wqkv[:, :, at:at + D], ACT.Copy, scale=DH ** -0.5)\
                        .then_inc(q_scaled, 1)
                if ly == 0:
                    act.wait_ge(q_scaled, 1)
                if ly == 0:
                    std(0)
                with act.Fori(0, B) as b:
                    b16 = b * TT
                    turn_out(ly, b16, TT)
                    for kind, i in PROJECTIONS:
                        if kind == "v" and ly:
                            act.wait_ge(v_mm, upto(1, ly, b16, i + 1))
                            act.activation(v_all[:, i, :], ring(2 * JOBS.index((kind, i)))[:, 0:D], ACT.Copy)\
                                .then_inc(v_ready, 1)
                        if kind == "q":
                            if i % (2 * NQ) >= ly:
                                part1(ly, b16, i - ly)
                            if i % (2 * NQ) >= ly + 1:
                                part2(ly, b16, i - ly - 1)
                            if i % (2 * NQ) == 2 * NQ - 1:
                                for k in range(i - ly + 1, i + 1):
                                    part2(ly, b16, k - 1)
                                    part1(ly, b16, k)
                                part2(ly, b16, i)
                    act.wait_ge(qk_split, upto(1, ly, b16, TT))
                    for n in range(ROT):
                        exp_block(ly, b16, 0, 0, n, True)
                    with act.Fori(0, H // GROUP - 1) as i:
                        hb = b16 + GROUP * i
                        for j in range(GROUP):
                            head(ly, hb, j, j, True, None)
                    for j in range(GROUP):
                        h = H - GROUP + j
                        head(ly, b16, h, j, h + 1 < H, b + (ly * (B + 1) + 1))
                    for t in range(TT):
                        act.wait_ge(ot_mm, upto(1, ly, b16, t + 1))
                        if t >= 4:
                            act.wait_ge(y_mm, upto(1, ly, b16, t - 3))
                        act.activation(o_t[:, t % 4, :], ps_m[:, t % MBANKS, 0:D], ACT.Copy).then_inc(ot_out, 1)
                if ly == 0:
                    std(B + 1)

                def turn_slots(i, s):
                    act.wait_ge(xs_turned, i + (ly * ETILES + 1))
                    act.activation(xsT[:, s, :, :], ps_m[:, s, :].rearrange("p (k n) -> p k n", k=KD), ACT.Copy)\
                        .then_inc(xsT_ready, 1)

                def hidden(i, s, more):
                    for f in range(NF):
                        act.wait_ge(h_mm, i * NF + (ly * ETILES * NF + f + 1))
                        act.activation(hid[:, f, :], ring(f)[:, 0:ET], ACT.Gelu).then_inc(gelu_out, 1)
                    if more:
                        turn_slots(i + 1, 1 - s)

                turn_slots(0, 0)
                with act.Fori(0, ETILES // 2) as ip:
                    for s in range(2):
                        hidden(2 * ip + s, s, True)
                hidden(ETILES - 1, 0, False)

        @block.tensor
        def _(pe):
            pe.wait_ge(consts_in, CONSTS)
            pe.wait_ge(pool_step, 2)
            pe.sem_inc(stack_free, SLOTS)
            for done in (acc_out, sum_mm, o_norm, x_stored, ys_out):
                pe.sem_inc(done, 1)
            for done in ys_stored:
                pe.sem_inc(done, 16)
            pe.wait_ge(onehot_ready, 3)
            for i, w in enumerate((tri, all_ones)):
                mm = pe.matmul(ps_o[:, i * P:(i + 1) * P], w, onehot.rearrange("p e j -> p (e j)"),
                               start=True, stop=True)
            mm.then_inc(ranks_mm, 1)

            def turn_xn(ly, b16, n):
                for t in range(n):
                    pe.wait_ge(xn_ready, b16 + (ly * (B + 1) * TT + t + 1))
                    if t >= MBANKS:
                        pe.wait_ge(xT_ready, turned(ly, b16, t - MBANKS + 1))
                    for k in range(KD):
                        mm = pe.transpose(ps_m[:, t % MBANKS, k * P:(k + 1) * P], xn[:, t, k * P:(k + 1) * P],
                                          identf[:, :])
                    mm.then_inc(xn_turned, 1)

            def project(ly, b16, job):
                kind, i = JOBS[job]
                back = (4, 2)[ly]
                if job >= back:
                    pe.wait_ge(*freed(ly, b16, *JOBS[job - back]))
                if kind == "v":
                    to = ring(job * (1, 2)[ly])
                    for k in range(KD):
                        mm = pe.matmul(to[:, 0:D], xT[:, k, i * P:(i + 1) * P], wqkv[:, k, 2 * D:3 * D],
                                       start=(k == 0), stop=(k == KD - 1))
                    mm.then_inc(v_mm, 1)
                    return
                half, proj, n = i // 8, i // 4 % 2, i % 4
                if half == proj == 0:
                    pe.wait_ge(xT_ready, turned(ly, b16, 4 * n + 4))
                outs = ((job, proj * D),) if ly == 0 else ((2 * job, proj * D), (2 * job + 1, (3 + proj) * D))
                for bank, at in outs:
                    at += half * P
                    for k in range(KD):
                        mm = pe.matmul(ring(bank), wqkv[:, k, at:at + P], xT[:, k, n * QW:(n + 1) * QW],
                                       start=(k == 0), stop=(k == KD - 1))
                mm.then_inc(qk_mm, 1)

            def item(ly, hb, h, at, what, slot):
                before = item_count(ly, hb, h, at)
                bank = (len(FIRST_STREAM) * (h is not None) + at) % MBANKS
                nxt = 0 if h is None else h + 1
                if what in (LO, HI):
                    g, of = (1, h) if what == LO else (0, nxt)
                    pe.wait_ge(c_ready, upto(2, ly, hb, of, g + 1))
                if h is not None or at >= MBANKS:
                    pe.wait_ge(item_used, before - MBANKS + 1)
                if what in (LO, HI):
                    pe.transpose(c_ps[bank][0:3 * TT // 2, :], cpart[:, g, :, :].rearrange("p i t -> p (i t)"),
                                 identb[:, :]).then_inc(item_mm, 1)
                    return
                qb, kc, w = UNIT[what]
                rows = c_row[ly]
                if what == 0:
                    pe.wait_ge(stack_in[slot], stack_count(ly, hb, nxt, slot))
                pe.matmul(ps_m[:, bank, 0:w], q_stack(slot)[0:rows, qb * P:(qb + 1) * P],
                          k_stack(slot)[0:rows, kc * QW:kc * QW + w], start=True, stop=True).then_inc(item_mm, 1)

            def stack_count(ly, hb, h, slot):
                per_a, per_b = 16 * (LOADS + 2), 16 * LOADS
                per = (per_a, per_b)[ly]
                before = per_a * B * (H // SLOTS) if ly else 0
                return hb * (per // SLOTS) + (before + per // SLOTS * (h - slot) + per)

            def rows_count(ly, hb, h, slot):
                per = 16 * 3
                return hb * (per // SLOTS) + per // SLOTS * (ly * B * H + h - slot + SLOTS)

            def scores(ly, hb, h, n, slot, opening):
                qt, kb, q0 = BLOCK[n]
                rows = c_row[ly] + 3
                bank, back = s_bank(slot, n)
                if n == 0:
                    pe.wait_ge(rows_in[0][slot], rows_count(ly, hb, h, slot))
                if n == FIRST_LO:
                    pe.wait_ge(rows_in[1][slot], rows_count(ly, hb, h, slot))
                if not opening or n >= 3:
                    pe.wait_ge(exp_done, upto(BLOCKS, ly, hb, h, n - back + 1))
                mm = pe.matmul(ps_s[:, bank, q0:QW], k_stack(slot)[0:rows, kb * P:(kb + 1) * P],
                               q_stack(slot)[0:rows, qt * QW + q0:(qt + 1) * QW], start=True, stop=True)
                if kb >= 4 * qt:
                    mm = pe.matmul(ps_s[:, bank, q0:q0 + P], identb[:, :], early[:, :], start=False, stop=True,
                                   skip_group_check=True)
                mm.then_inc(s_mm, 1)

            def times_v(ly, hb, h, g, slot):
                fresh = g in FIRST_GROUP
                if fresh:
                    pe.wait_ge(acc_out, upto(NQ, ly, hb, h, NQ - FIRST_GROUP[g]))
                if g == GROUPS - 1:
                    pe.matmul(ps_acc[:, :], zeros[0:P // 2, :], q_stack(slot)[0:P // 2, 0:QW], start=True, stop=False,
                              skip_group_check=True).then_inc(stack_free, 1)
                    fresh = False
                pe.wait_ge(exp_done, upto(BLOCKS, ly, hb, h, 4 * g + 4))
                if g == 0:
                    pe.wait_ge(v_head_ready, upto(1, ly, hb, h, 1))
                pieces = [(r, r, BLOCK[4 * g + r][2], QW) for r in range(4)]
                if g in LAST_GROUP:
                    pieces[0] = (0, 0, 0, QW - P)
                    pieces.append((0, 3, QW - P, QW))
                for r, tile, lo, hi in pieces:
                    n = 4 * g + r
                    _, kb, q0 = BLOCK[n]
                    mm = pe.matmul(ps_acc[32 * tile:32 * tile + 32, lo:hi], v_head[:, slot % 2, kb, :],
                                   probs[:, n % 8, lo - q0:hi - q0], start=fresh, stop=g in LAST_GROUP,
                                   skip_group_check=True)
                mm.then_inc(pv_mm, 1)

            def sum_up(ly, hb, h):
                pe.wait_ge(acc_out, upto(NQ, ly, hb, h, NQ + 1))
                pe.wait_ge(o_norm, upto(1, ly, hb, h, 1))
                for qt in range(NQ):
                    mm = pe.matmul(ps_o[32 * qt:32 * qt + 32, :], sel[:, :], acc_sb[:, qt, :], start=True, stop=True)
                mm.then_inc(sum_mm, 1)

            def turn_sum(ly, hb, h):
                pe.wait_ge(sum_out, upto(1, ly, hb, h, 1))
                for c in range(4):
                    mm = pe.transpose(ps_o[:, c * P:(c + 1) * P], osum[:, c * P:(c + 1) * P], identf[:, :])
                mm.then_inc(o_mm, 1)

            def one_block(ly, hb, h, n, slot, more, opening):
                scores(ly, hb, h, n, slot, opening)
                at = item_at(more, n)
                for what in stream(more)[n]:
                    item(ly, hb, h, at, what, (slot + 1) % SLOTS)
                    at += 1
                if n >= PV_LAG and (n - PV_LAG) % 4 == 0:
                    times_v(ly, hb, h, (n - PV_LAG) // 4, slot)

            def head(ly, hb, h, slot, more, more2):
                for dh, n in steps_of(h):
                    if not dh:
                        one_block(ly, hb, h, n, slot, more, False)
                        continue
                    if more:
                        one_block(ly, hb, h + 1, n, (slot + 1) % SLOTS, more2, False)
                    if 4 * (GROUPS - 1) + PV_LAG - BLOCKS == n:
                        times_v(ly, hb, h, GROUPS - 1, slot)
                    if n == SUM_STEP:
                        sum_up(ly, hb, h)
                    if n == TURN_STEP:
                        turn_sum(ly, hb, h)

            for ly in range(2):
                pe.wait_ge(weights_in, 32 * (ly + 1))
                pe.wait_ge(q_scaled, (2, 4)[ly])
                pe.wait_ge(ones_in, 16 * SLOTS * (ly + 1))
                with pe.Fori(0, B) as b:
                    b16 = b * TT
                    turn_xn(ly, b16, TT)
                    job = 0
                    for kind, i in PROJECTIONS:
                        if kind == "m":
                            item(ly, b16, None, i, FIRST_STREAM[i], 0)
                        else:
                            project(ly, b16, job)
                            job += 1
                    pe.wait_ge(v_ready, upto(1, ly, b16, TT))
                    pe.wait_ge(*freed(ly, b16, "q", 4 * NQ - 1))
                    for n in range(ROT):
                        one_block(ly, b16, 0, n, 0, True, True)
                    with pe.Fori(0, H // GROUP - 1) as i:
                        hb = b16 + GROUP * i
                        for j in range(GROUP):
                            head(ly, hb, j, j, True, True)
                    for j in range(GROUP):
                        h = H - GROUP + j
                        head(ly, b16, h, j, h + 1 < H, h + 2 < H)
                    pe.wait_ge(o_norm, upto(1, ly, b16, H, 1))
                    for t in range(TT + 2):
                        if t < TT:
                            if t >= MBANKS:
                                pe.wait_ge(ot_out, upto(1, ly, b16, t - MBANKS + 1))
                            for k in range(KD):
                                mm = pe.transpose(ps_m[:, t % MBANKS, k * P:(k + 1) * P], oh[:, t, k * P:(k + 1) * P],
                                                  identf[:, :])
                            mm.then_inc(ot_mm, 1)
                        if t >= 2:
                            pe.wait_ge(ot_out, upto(1, ly, b16, t - 1))
                            if t - 2 >= 4:
                                pe.wait_ge(y_added, upto(1, ly, b16, t - 5))
                            for k in range(KD):
                                mm = pe.matmul(ring(t - 2)[:, 0:D], o_t[:, (t - 2) % 4, k * P:(k + 1) * P],
                                               wo[:, k, :], start=(k == 0), stop=(k == KD - 1))
                            mm.then_inc(y_mm, 1)
                    pe.wait_ge(y_added, upto(1, ly, b16, TT))

                def turn_slots(i, s):
                    pe.wait_ge(xs_in[s], (i - s) * 8 + (ly * 16 * ((ETILES + 1 - s) // 2) + 16))
                    for k in range(KD):
                        for c in range(2):
                            mm = pe.transpose(ps_m[:, s, k * ET + c * P:k * ET + (c + 1) * P],
                                              xs_sb[:, s, c, k * P:(k + 1) * P], identf[:, :])
                    mm.then_inc(xs_turned, 1)

                def expert_tile(i, s, more):
                    pe.wait_ge(ew_in[s], (i - s) * 16 + (ly * 32 * ((ETILES + 1 - s) // 2) + 32))
                    pe.wait_ge(xsT_ready, i + (ly * ETILES + 1))
                    for f in range(NF):
                        if f >= 4:
                            pe.wait_ge(gelu_out, i * NF + (ly * ETILES * NF + f - 3))
                        for k in range(KD):
                            mm = pe.matmul(ring(f)[:, 0:ET], w1_sb[:, s, k, f * P:(f + 1) * P], xsT[:, s, k, :],
                                           start=(k == 0), stop=(k == KD - 1))
                        mm.then_inc(h_mm, 1)
                    if more:
                        turn_slots(i + 1, 1 - s)
                    pe.wait_ge(ys_out, 2 * i + (ly * 2 * ETILES + 1))
                    for c in range(2):
                        for f in range(NF):
                            if c == 0:
                                pe.wait_ge(gelu_out, i * NF + (ly * ETILES * NF + f + 1))
                            mm = pe.matmul(y_bank[c], hid[:, f, c * P:(c + 1) * P], w2_sb[:, s, f, :],
                                           start=(f == 0), stop=(f == NF - 1))
                        mm.then_inc(fy_mm, 1)

                turn_slots(0, 0)
                with pe.Fori(0, ETILES // 2) as ip:
                    for s in range(2):
                        expert_tile(2 * ip + s, s, True)
                expert_tile(ETILES - 1, 0, False)
                pe.wait_ge(ys_out, (ly + 1) * 2 * ETILES + 1)

        @block.vector
        def _(dve):
            dve.memset(part_max[:, :, :], LOWEST).then_inc(dve_step, 1)
            dve.wait_ge(consts_in, CONSTS)
            count = 1

            def done(ins):
                nonlocal count
                ins.then_inc(dve_step, 1)
                count += 1
                dve.wait_ge(dve_step, count)

            done(dve.tensor_copy(choice, eix[:, :, :].rearrange("p t k -> p (t k)")))
            dve.memset(all_ones, 1.0).then_inc(onehot_ready, 1)
            dve.memset(before[:, :, 0], 0.0).then_inc(onehot_ready, 1)
            for e in range(E):
                mm = dve.tensor_scalar(onehot[:, e, :], choice, float(e), 1.0, ALU.is_equal, ALU.mult)
            mm.then_inc(onehot_ready, 1)
            ranks = ps_o[:, 0:P].rearrange("p (e j) -> p e j", e=E)
            totals = ps_o[:, P:2 * P].rearrange("p (e j) -> p e j", e=E)
            dve.wait_ge(ranks_mm, 1)
            for j in range(1, J):
                done(dve.tensor_tensor(before[:, :, j], before[:, :, j - 1], totals[:, :, j - 1], ALU.add))
            done(dve.tensor_tensor(n_of, before[:, :, J - 1], totals[:, :, J - 1], ALU.add))
            done(dve.tensor_scalar(tiles_of, n_of, 0.0, 1.0, ALU.is_gt, ALU.mult))
            for i in range(1, FT * TOPK // ET):
                done(dve.scalar_tensor_tensor(out=tiles_of, in0=n_of, scalar=float(i * ET), in1=tiles_of,
                                              op0=ALU.is_gt, op1=ALU.add))
            done(dve.tensor_copy(tiles_to, tiles_of))
            for e in range(1, E):
                done(dve.tensor_tensor(tiles_to[:, e:e + 1], tiles_to[:, e - 1:e], tiles_of[:, e:e + 1], ALU.add))
            done(dve.tensor_tensor(base_of, tiles_to, tiles_of, ALU.subtract))
            done(dve.tensor_scalar(base_of, base_of, float(ET), 1.0, ALU.mult, ALU.mult))
            done(dve.tensor_tensor(rank, ranks, before, ALU.add))
            done(dve.tensor_tensor(rank, rank, base_of.rearrange("p (e o) -> p e o", o=1).broadcast_to([P, E, J]),
                                   ALU.add))
            done(dve.tensor_tensor(rank, rank, onehot, ALU.mult))
            done(dve.tensor_reduce(slot_f, rank.rearrange("p e j -> p j e"), AX_X, ALU.add))
            dve.tensor_copy(slot_of[:, :], slot_f).then_inc(table_ready, 1)
            done(dve.memset(expert_f, 0.0))
            for e in range(E):
                done(dve.scalar_tensor_tensor(out=expert_f, in0=ramp, scalar=tiles_to[:, e:e + 1], in1=expert_f,
                                              op0=ALU.is_ge, op1=ALU.add))
            done(dve.tensor_scalar(expert_f, expert_f, float(E - 1), 1.0, ALU.min, ALU.mult))
            dve.tensor_copy(expert_of[:, :], expert_f).then_inc(table_ready, 1)
            dve.wait_ge(table_ready, 2)
            setup_steps = count
            ln_steps = 6

            def norm(nth):
                def base(k):
                    return nth * ln_steps + (setup_steps + k)

                dve.wait_ge(xn_in, nth * 16 + 16)
                for t in range(TT):
                    mm = dve.bn_stats(stats[:, t, :], xn[:, t, :])
                mm.then_inc(dve_step, 1)
                dve.wait_ge(dve_step, base(1))
                dve.sem_inc(passed, 1)
                for t in range(TT):
                    mm = dve.bn_aggr(mv[:, t, :], stats[:, t, :])
                mm.then_inc(dve_step, 1)
                dve.wait_ge(dve_step, base(2))
                dve.tensor_scalar_add(vpe[:, :], mv[:, :, 1], EPS).then_inc(var_ready, 1)
                dve.wait_ge(sd_ready, nth + 1)
                dve.reciprocal(r0[:, :], sd[:, :]).then_inc(dve_step, 1)
                dve.wait_ge(dve_step, base(3))
                dve.tensor_tensor(r1[:, :], r0[:, :], r0[:, :], ALU.mult).then_inc(dve_step, 1)
                dve.wait_ge(dve_step, base(4))
                dve.tensor_tensor(r1[:, :], r1[:, :], vpe[:, :], ALU.mult).then_inc(dve_step, 1)
                dve.wait_ge(dve_step, base(5))
                dve.tensor_scalar(r1[:, :], r1[:, :], -0.5, 1.5, ALU.mult, ALU.add).then_inc(dve_step, 1)
                dve.wait_ge(dve_step, base(6))
                dve.tensor_tensor(rstd[:, :], r0[:, :], r1[:, :], ALU.mult).then_inc(rstd_out, 1)
                dve.wait_ge(rstd_out, nth + 1)
                for t in range(TT):
                    dve.tensor_scalar(xn[:, t, :], xn[:, t, :], mv[:, t, 0:1], rstd[:, t:t + 1],
                                      ALU.subtract, ALU.mult).then_inc(xn_ready, 1)

            def use_item(ly, hb, h, at, what):
                before = item_count(ly, hb, h, at)
                bank = (len(FIRST_STREAM) * (h is not None) + at) % MBANKS
                dve.wait_ge(item_mm, before + 1)
                if what in (LO, HI):
                    g = (1, 0)[what == HI]
                    dve.tensor_copy(crow[:, g, :], c_ps[bank][0:3 * TT // 2, :]).then_inc(item_used, 1)
                    return
                qb, kc, w = UNIT[what]
                if kc == qb // 4:
                    dve.sem_inc(passed, 1)
                    dve.tensor_tensor_reduce(ps_m[:, bank, 0:w], ps_m[:, bank, 0:w], mask[:, QW - w:QW], 1.0, LOWEST,
                                             ALU.add, ALU.max, part_max[:, qb, kc:kc + 1]).then_inc(item_used, 1)
                else:
                    dve.reduce_max(part_max[:, qb, kc:kc + 1], ps_m[:, bank, 0:w], AX_X).then_inc(item_used, 1)
                if what + 1 in (HI_UNITS, UNITS):
                    g = (HI_UNITS, UNITS).index(what + 1)
                    cols = (slice(TT // 2, TT), slice(0, TT // 2))[g]
                    dve.wait_ge(item_used, before + 1)
                    dve.tensor_reduce(negmax[:, cols], part_max[:, cols, :], AX_X, ALU.max, negate=True)\
                        .then_inc(m_ready, 1)

            def beside(ly, hb, h, more, n):
                at = item_at(more, n)
                for what in stream(more)[n]:
                    use_item(ly, hb, h, at, what)
                    at += 1

            def normalise(ly, hb, h, col):
                o = ps_o[:, :].rearrange("p (c q d) -> p q c d", c=4, q=NQ)
                dve.wait_ge(o_mm, upto(1, ly, hb, h, 1))
                dve.reciprocal(recip[:, :, :], o[:, :, :, DH]).then_inc(recip_out, 1)
                dve.wait_ge(recip_out, upto(1, ly, hb, h, 1))
                dve.tensor_tensor(oh[:, :, bass.ds(col, DH)].rearrange("p (q c) d -> p q c d", c=4), o[:, :, :, 0:DH],
                                  recip[:, :, :].rearrange("p q (c o) -> p q c o", o=1).broadcast_to([P, NQ, 4, DH]),
                                  ALU.mult).then_inc(o_norm, 1)

            def head(ly, hb, h, more, more2, col, nth):
                if not more:
                    for n in range(ROT, BLOCKS):
                        beside(ly, hb, h, more, n)
                    norm(nth)
                for dh, n in steps_of(h):
                    if dh and more:
                        beside(ly, hb, h + 1, more2, n)
                    if not dh and more:
                        beside(ly, hb, h, more, n)
                normalise(ly, hb, h, col)

            def rotate(b16, u):
                n = u % 4
                cols = slice(n * QW, (n + 1) * QW)
                job = JOBS.index(("q", u))
                dve.wait_ge(qk_mm, upto(1, 1, b16, u + 1))
                if u >= 2:
                    dve.wait_ge(roped, b16 + (u - 1))
                dve.tensor_tensor(rot1[:, u % 2, :], ring(2 * job), cosb[:, cols], ALU.mult)
                dve.tensor_tensor(rot2[:, u % 2, :], ring(2 * job + 1), sinb[:, cols], ALU.mult).then_inc(rotated, 1)

            def place(u, i):
                half, proj, n = u // 8, u // 4 % 2, u % 4
                return part(proj, half, i)[:, n * QW:(n + 1) * QW]

            def rest(ly, b16, u):
                half, proj = u // 8, u // 4 % 2
                dve.wait_ge(part1_out, upto(1, ly, b16, u + 1))
                if u >= 2:
                    dve.wait_ge(qk_split, upto(1, ly, b16, u - 1))
                if ly == 0:
                    dve.scalar_tensor_tensor(out=res[:, u % 2, :], in0=ring(JOBS.index(("q", u))),
                                             scalar=bqk[:, proj, half:half + 1], in1=place(u, 0),
                                             op0=ALU.add, op1=ALU.subtract).then_inc(res_out, 1)
                else:
                    dve.tensor_tensor(res[:, u % 2, :], qf[:, u % 2, :], place(u, 0), ALU.subtract)\
                        .then_inc(res_out, 1)

            def part3(b16, u):
                dve.wait_ge(part2_out, upto(1, 1, b16, u + 1))
                dve.tensor_tensor(place(u, 2), res[:, u % 2, :], place(u, 1), ALU.subtract).then_inc(qk_split, 1)

            norm(0)
            for ly in range(2):
                with dve.Fori(0, B) as b:
                    b16 = b * TT
                    for kind, i in PROJECTIONS:
                        if kind == "m":
                            use_item(ly, b16, None, i, FIRST_STREAM[i])
                        elif kind == "v" and ly == 0:
                            dve.wait_ge(v_mm, upto(1, ly, b16, i + 1))
                            dve.tensor_tensor(v_all[:, i, :], ring(JOBS.index((kind, i)))[:, 0:D], bv_bc, ALU.add)\
                                .then_inc(v_ready, 1)
                        elif kind == "q" and ly == 0:
                            rest(ly, b16, i)
                        elif kind == "q":
                            rotate(b16, i)
                            if i % 8 >= 1:
                                rest(ly, b16, i - 1)
                            if i % 8 >= 2:
                                part3(b16, i - 2)
                            if i % 8 == 7:
                                part3(b16, i - 1)
                                rest(ly, b16, i)
                                part3(b16, i)
                    for n in range(ROT):
                        beside(ly, b16, 0, True, n)
                    with dve.Fori(0, H // GROUP - 1) as i:
                        hb = b16 + GROUP * i
                        for j in range(GROUP):
                            head(ly, hb, j, True, True, DH * GROUP * i + DH * j, None)
                    for h in range(H - GROUP, H):
                        head(ly, b16, h, h + 1 < H, h + 2 < H, DH * h, b + (ly * (B + 1) + 1))
                    dve.wait_ge(xb_in, 16 * (b + 1) + 16 * ly * (B + 1))
                    for t in range(TT + 1):
                        if t < TT:
                            dve.wait_ge(y_mm, upto(1, ly, b16, t + 1))
                            dve.tensor_tensor(xb[:, t, :], xb[:, t, :], ring(t)[:, 0:D], ALU.add)\
                                .then_inc(y_added, 1)
                        if ly == 0 and t >= 1:
                            dve.wait_ge(y_added, upto(1, ly, b16, t))
                            dve.tensor_tensor(xb[:, t - 1, :], xb[:, t - 1, :], bo_bc, ALU.add)\
                                .then_inc(x_ready, 1)

                if ly == 0:
                    norm(B + 1)
                dve.wait_ge(xb_in, 16 * (ly + 1) * (B + 1))
                for t in range(NFT):
                    dve.tensor_tensor(xb[:, t, :], xb[:, t, :], fb_bc[:, :], ALU.add).then_inc(mixed, 1)

                def ys_tile(i, s):
                    for c in range(2):
                        dve.wait_ge(fy_mm, 2 * i + (ly * 2 * ETILES + c + 1))
                        if c == 0:
                            dve.wait_ge(ys_stored[s], (i - s) * 8 + (ly * 16 * ((ETILES + 1 - s) // 2) + 16))
                        dve.tensor_copy(ys_sb[:, s, c, :], y_bank[c]).then_inc(ys_out, 1)

                with dve.Fori(0, ETILES // 2) as ip:
                    for s in range(2):
                        ys_tile(2 * ip + s, s)
                ys_tile(ETILES - 1, 0)
                for k in range(TOPK):
                    for t in range(NFT):
                        dve.wait_ge(picked_in[k], 16 * NFT * (ly + 1))
                        dve.wait_ge(mixed, ly * TOPK * NFT + k * NFT + t + 1)
                        dve.scalar_tensor_tensor(out=xb[:, t, :], in0=picked[:, t * TOPK + k, :],
                                                 scalar=ewt[:, t, k:k + 1], in1=xb[:, t, :],
                                                 op0=ALU.mult, op1=ALU.add).then_inc((mixed, ffn_out)[k], 1)


def kernel(**inputs):
    import ml_dtypes
    import concourse.bacc as bacc
    from concourse.bass_utils import run_bass_kernel_spmd as run

    bf = ml_dtypes.bfloat16
    g = {k: np.asarray(v) for k, v in inputs.items()}
    x = np.roll(g["L0_attn_a_x"], ROUTED, axis=0).reshape(B * L, D)
    w_a = np.concatenate([g["L0_attn_a_Wq"].T, g["L0_attn_a_Wk"].T, g["L0_attn_a_Wv"].T], axis=1)
    kqv = g["L0_attn_b_W_KQV"]
    wk, wq, wv = kqv[0:D], kqv[D:2 * D], kqv[2 * D:]
    swap = np.arange(D) ^ 1
    w_b = np.concatenate([wq.T, wk.T, wv.T, wq[swap].T, wk[swap].T], axis=1)
    bqk = np.stack([g["L0_attn_a_bq"].reshape(KD, P).T, g["L0_attn_a_bk"].reshape(KD, P).T], axis=1)

    pos = np.arange(L)
    inv = (1.0 / np.float32(10000.0) ** (np.arange(0, DH, 2, dtype=np.float32) / np.float32(DH))).astype(np.float32)
    freqs = (pos.astype(np.float32)[:, None] * inv[None, :]).astype(np.float32)
    feat = np.arange(P) % DH
    cos_t = np.cos(freqs).astype(np.float32)[:, feat // 2].T
    sin_t = (np.sin(freqs).astype(np.float32)[:, feat // 2] * np.where(feat % 2, 1, -1)).T.astype(np.float32)
    slopes = np.power(np.float32(2.0), (np.float32(-8.0) * np.arange(1, H + 1, dtype=np.float32) / np.float32(H)))
    slopes = slopes.astype(np.float32)
    cut, rest = [], slopes.copy()
    for _ in range(3):
        s = rest.astype(bf)
        cut.append(s.astype(np.float32))
        rest = (rest - cut[-1]).astype(np.float32)
    q_pos = np.zeros((H, POS, L), np.float32)
    k_pos = np.zeros((H, POS, L), np.float32)
    for i in range(3):
        for u, p in enumerate((pos // P * P, pos % P)):
            q_pos[:, 4 * i + 2 * u] = p
            k_pos[:, 4 * i + 2 * u] = -cut[i][:, None]
            q_pos[:, 4 * i + 2 * u + 1] = cut[i][:, None]
            k_pos[:, 4 * i + 2 * u + 1] = p
    eye = np.eye(P, dtype=np.float32)
    r, c = np.arange(P)[:, None], np.arange(P)[None, :]
    mask = np.zeros((P, QW), np.float32)
    mask[:, QW - P:] = np.where(c > r, MASKED, 0.0)
    early = np.where(r > c, MASKED, 0.0)
    sel = np.zeros((P, 2 * DH), np.float32)
    for q in range(4):
        for d in range(DH + 1):
            sel[2 * DH * q + d, d] = 1.0

    def rows(v):
        return np.ascontiguousarray(np.broadcast_to(v[None, :], (P, D)))

    arrays = {
        "x_in": x, "w_a": w_a, "wo_a": g["L0_attn_a_Wo"].T, "bqk_a": bqk, "bv_a": rows(g["L0_attn_a_bv"]),
        "bo_a": rows(g["L0_attn_a_bo"]), "w_b": w_b, "wo_b": g["L0_attn_b_W_O"].T, "cos_t": cos_t, "sin_t": sin_t,
        "q_pos": q_pos.astype(bf), "k_pos": k_pos.astype(bf), "ones_rows": np.ones((3, L), bf),
        "ident_f": eye, "ident_b": eye.astype(bf), "late_keys": mask.astype(bf), "early_queries": early.astype(bf), "sel_in": sel,
        "tri_in": np.triu(eye * 0 + 1, 1).astype(np.float32),
        "ramp_in": np.ascontiguousarray(np.broadcast_to(np.arange(ETILES, dtype=np.float32), (P, ETILES))),
        "e_w": g["L0_ffn_expert_weights"], "e_idx": g["L0_ffn_expert_indices"],
        "w1": g["L0_ffn_w1"], "w2": g["L0_ffn_w2"], "fbias": rows(g["L0_ffn_bias"]),
    }
    nc = bacc.Bacc("TRN2", target_bir_lowering=False, num_devices=1)
    aps, maps = {}, {}
    for name, a in arrays.items():
        a = np.ascontiguousarray(a)
        maps[name + "_dram"] = a
        aps[name] = nc.dram_tensor(name + "_dram", a.shape, mybir.dt.from_np(a.dtype), kind="ExternalInput").ap()
    aps["ident_in"] = (aps.pop("ident_f"), aps.pop("ident_b"))
    aps["mask_in"] = (aps.pop("late_keys"), aps.pop("early_queries"))
    aps["out"] = nc.dram_tensor("out_dram", (B * L, D), F32, kind="ExternalOutput").ap()
    build(nc, **aps)
    res = run(nc, [maps], core_ids=[0])
    return np.roll(res.results[0]["out_dram"].reshape(B, L, D), -ROUTED, axis=0)
```
